# Optimizing a Trainium2 kernel written in Bass

```python
import numpy as np
import jax
import jax.numpy as jnp

def _softmax(x, axis=-1):
    return jax.nn.softmax(x, axis=axis)

def _gelu(x):
    return jax.nn.gelu(x, approximate=True)

def _silu(x):
    return jax.nn.silu(x)

def _sigmoid(x):
    return jax.nn.sigmoid(x)

def _layernorm(x, axis=-1, eps=1e-05):
    m = jnp.mean(x, axis=axis, keepdims=True)
    v = jnp.var(x, axis=axis, keepdims=True)
    return (x - m) / jnp.sqrt(v + eps)

def _scatter_add(tgt, idx, src, axis=0):
    return tgt.at[idx].add(src)

def _segment_sum(src, seg, n):
    return jax.ops.segment_sum(src, seg, n)
kernel_name = 'mk_flamingo_gated_d1_seqx_r8_4a287d'

def setup_inputs(seed: int=0):
    np.random.seed(seed)
    _w = jnp.asarray

    def _rec_inputs():
        import jax
        import jax.numpy as jnp
        _rk = jax.random.key(seed)
        x = 0.0003765 + 1 * jax.random.normal(jax.random.fold_in(_rk, 1), (8, 128, 256), jnp.float32)
        _lenS = 128 - jax.random.randint(jax.random.fold_in(_rk, 7), (8,), 0, max(1, 128 // 4) + 1, jnp.int32)
        _lenS2 = 128 - jax.random.randint(jax.random.fold_in(_rk, 8), (8,), 0, max(1, 128 // 4) + 1, jnp.int32)
        _ctx_2048P = jax.random.normal(jax.random.fold_in(_rk, 11), (8, 16, 256), jnp.float32)
        _ctx_2048c = jax.random.dirichlet(jax.random.fold_in(_rk, 511), 0.3 * jnp.ones((16,), jnp.float32), (8, 128))
        _ctx_2048t = jnp.einsum('bsk,bkd->bsd', _ctx_2048c, _ctx_2048P)
        _ctx_2048t = _ctx_2048t * jax.lax.rsqrt(jnp.mean(jnp.square(_ctx_2048t)) + 1e-12) * 0.953939
        ctx_2048 = -0.000292821 + 1.00034 * (_ctx_2048t + 0.3 * jax.random.normal(jax.random.fold_in(_rk, 611), (8, 128, 256), jnp.float32))
        _g = jax.random.normal(jax.random.fold_in(_rk, 9001), (2, 1), jnp.float32)
        _g = jnp.sign(_g) * jnp.maximum(jnp.abs(_g), 1.0) + (_g == 0) * 1.0
        g_xattn = _g[0]
        g_ffn = _g[1]
        return (x, ctx_2048, g_xattn, g_ffn)
    x, ctx_2048, g_xattn, g_ffn = _rec_inputs()

    def _L0_xattn_setup():
        import jax, jax.numpy as jnp
        import numpy as np
        key = jax.random.key(seed)
        k1, k2, k3, k4, k5 = jax.random.split(key, 5)
        B, D_MODEL, L = (2, 128, 256)
        HEAD_DIM = 8
        H = D_MODEL // HEAD_DIM
        return {'k': jax.random.normal(k1, (B, D_MODEL, L), dtype=jnp.float32), 'v': jax.random.normal(k2, (B, D_MODEL, L), dtype=jnp.float32), 'q': jax.random.normal(k3, (B, D_MODEL, L), dtype=jnp.float32), 'ssm_kernel': jax.random.normal(k4, (H, L), dtype=jnp.float32), 'D': jax.random.normal(k5, (H,), dtype=jnp.float32), 'head_dim': HEAD_DIM}
    _L0_xattn_all = _L0_xattn_setup()
    _L0_xattn_in = {k: v for k, v in _L0_xattn_all.items() if k in ('ssm_kernel', 'D')}
    del _L0_xattn_all

    def _L0_ffn_setup():
        import math
        import jax, jax.numpy as jnp
        import numpy as np
        NUM_EXPERTS = 8
        TOP_K = 2
        CAP_FACTOR = 1.25
        D_MODEL = 256
        D_HIDDEN = 1024
        B, S = (4, 256)
        key = jax.random.key(seed)
        ks = jax.random.split(key, 6)
        x = jax.random.normal(ks[0], (B, S, D_MODEL), dtype=jnp.float32)
        gating_w = jax.random.normal(ks[1], (D_MODEL, NUM_EXPERTS), dtype=jnp.float32) * (1.0 / math.sqrt(D_MODEL))
        w1 = jax.random.normal(ks[2], (NUM_EXPERTS, D_MODEL, D_HIDDEN), dtype=jnp.float32) * (1.0 / math.sqrt(D_MODEL))
        b1 = jnp.zeros((NUM_EXPERTS, D_HIDDEN), dtype=jnp.float32)
        w2 = jax.random.normal(ks[3], (NUM_EXPERTS, D_HIDDEN, D_MODEL), dtype=jnp.float32) * (1.0 / math.sqrt(D_HIDDEN))
        b2 = jnp.zeros((NUM_EXPERTS, D_MODEL), dtype=jnp.float32)
        return {'x': x, 'gating_w': gating_w, 'w1': w1, 'b1': b1, 'w2': w2, 'b2': b2}
    _L0_ffn_all = _L0_ffn_setup()
    _L0_ffn_in = {k: v for k, v in _L0_ffn_all.items() if k in ('gating_w', 'w1', 'b1', 'w2', 'b2')}
    del _L0_ffn_all
    return {'x': x, 'ctx_2048': ctx_2048, 'g_xattn': g_xattn, 'g_ffn': g_ffn, 'L0_xattn_ssm_kernel': _L0_xattn_in['ssm_kernel'], 'L0_xattn_D': _L0_xattn_in['D'], 'L0_ffn_gating_w': _L0_ffn_in['gating_w'], 'L0_ffn_w1': _L0_ffn_in['w1'], 'L0_ffn_b1': _L0_ffn_in['b1'], 'L0_ffn_w2': _L0_ffn_in['w2'], 'L0_ffn_b2': _L0_ffn_in['b2']}

def reference(x, ctx_2048, g_xattn, g_ffn, L0_xattn_ssm_kernel, L0_xattn_D, L0_ffn_gating_w, L0_ffn_w1, L0_ffn_b1, L0_ffn_w2, L0_ffn_b2):
    import jax
    import jax.numpy as jnp

    def _L0_xattn_ref(k, v, q, ssm_kernel, D, head_dim):
        import jax, jax.numpy as jnp
        import numpy as np
        B, HD, L = k.shape
        H = HD // head_dim
        fft_size = 2 * L
        k_ = k.reshape(B, H, head_dim, L)
        v_ = v.reshape(B, H, head_dim, L)
        q_ = q.reshape(B, H, head_dim, L)
        kv = jnp.einsum('bhil,bhjl->bijhl', k_, v_)
        kv_f = jnp.fft.rfft(kv, n=fft_size)
        kernel_f = jnp.fft.rfft(ssm_kernel, n=fft_size)
        y = jnp.fft.irfft(kv_f * kernel_f, n=fft_size)[..., :L]
        out = y + kv * D[None, None, None, :, None]
        out = jnp.einsum('bijhl,bhil->bjhl', out, q_)
        out = jnp.transpose(out, (0, 2, 1, 3)).reshape(B, H * head_dim, L)
        return out.astype(k.dtype)

    def _L0_ffn_ref(x, gating_w, w1, b1, w2, b2):
        import math
        import jax, jax.numpy as jnp
        import numpy as np
        NUM_EXPERTS = 8
        TOP_K = 2
        CAP_FACTOR = 1.25
        D_MODEL = 256
        D_HIDDEN = 1024
        B, S = (4, 256)
        b, s, d = x.shape
        x_flat = x.reshape(-1, d)
        T = x_flat.shape[0]
        num_items = T * TOP_K
        capacity = int(math.ceil(num_items / NUM_EXPERTS * CAP_FACTOR))
        gates = jax.nn.softmax(x_flat @ gating_w, axis=-1)
        topk_w, topk_idx = jax.lax.top_k(gates, TOP_K)
        norm_w = topk_w / (jnp.sum(topk_w, axis=-1, keepdims=True) + 1e-08)
        flat_e = topk_idx.reshape(-1)
        flat_t = jnp.repeat(jnp.arange(T, dtype=jnp.int32), TOP_K)
        flat_w = norm_w.reshape(-1)
        onehot = (flat_e[:, None] == jnp.arange(NUM_EXPERTS)[None, :]).astype(jnp.int32)
        pos_all = jnp.cumsum(onehot, axis=0) - 1
        position = jnp.take_along_axis(pos_all, flat_e[:, None].astype(jnp.int32), axis=1)[:, 0]
        valid = position < capacity
        pos_scatter = jnp.where(valid, position, capacity)
        buf = jnp.zeros((NUM_EXPERTS, capacity, d), dtype=x.dtype)
        buf = buf.at[flat_e, pos_scatter].set(x_flat[flat_t], mode='drop')
        h = jnp.maximum(jnp.einsum('ecd,edh->ech', buf, w1) + b1[:, None, :], 0.0)
        out_e = jnp.einsum('ech,ehd->ecd', h, w2) + b2[:, None, :]
        pos_gather = jnp.minimum(position, capacity - 1)
        gathered = out_e[flat_e, pos_gather]
        w_eff = jnp.where(valid, flat_w, 0.0)
        out_flat = jnp.zeros_like(x_flat).at[flat_t].add(gathered * w_eff[:, None])
        return out_flat.reshape(b, s, d)
    x = x + jnp.tanh(g_xattn[0]) * _L0_xattn_ref(ctx_2048, ctx_2048, _layernorm(x, axis=-1), L0_xattn_ssm_kernel, L0_xattn_D, 8)
    x = x + jnp.tanh(g_ffn[0]) * _L0_ffn_ref(_layernorm(x, axis=-1), L0_ffn_gating_w, L0_ffn_w1, L0_ffn_b1, L0_ffn_w2, L0_ffn_b2)
    return x

_drawn_inputs = setup_inputs


def setup_inputs(seed=0):
    import zlib

    import numpy as np

    out = dict(_drawn_inputs(seed))
    spreads = {'L0_ffn_b1': (0.0, 0.8), 'L0_ffn_b2': (0.0, 2.0)}
    factors = {'L0_ffn_gating_w': 3.597, 'L0_ffn_w1': 3.887, 'L0_ffn_w2': 3.213}
    for name, (base, spread) in spreads.items():
        noise = np.random.default_rng([zlib.crc32(name.encode()), seed]).standard_normal(out[name].shape)
        drawn = base * np.exp(spread * noise) if base else spread * noise
        out[name] = jnp.asarray(drawn.astype(out[name].dtype))
    for name, factor in factors.items():
        out[name] = (out[name] * factor).astype(out[name].dtype)
    return out
```

```python
from contextlib import ExitStack

import concourse.bass as bass
from concourse import mybir

F32 = mybir.dt.float32
F32R = mybir.dt.float32r
F16 = mybir.dt.float16
BF16 = mybir.dt.bfloat16
I32 = mybir.dt.int32
U32 = mybir.dt.uint32
ALU = mybir.AluOpType
ACT = mybir.ActivationFunctionType
AX_X = mybir.AxisListType.X

P = 128
HEAD_DIM = 8
TOP_K = 2
LN_EPS = 1e-5
NORM_EPS = 1e-8
OUT_OF_BOUNDS = 8192.0


def wait_for(engine, semaphore, value):
    if not isinstance(value, int) or value > 0:
        engine.wait_ge(semaphore, value)


def build_gated_block(nc, x, ctx, g_xattn, g_ffn, ssm_kernel, D_skip, gating_w, w1, b1, w2, b2, out):
    B, S, DM = x.shape
    H, L = ssm_kernel.shape
    E, _, HID = w1.shape
    HALVES = DM // P
    T = B * S
    CAP = -(-T * TOP_K * 5 // (E * 4))
    SLOTS = E * CAP
    TILES = SLOTS // P
    PAIRS = E // 2
    TPP = TILES // PAIRS
    CH = HID // P
    KVW = B * HEAD_DIM * HEAD_DIM
    HEAD_RING = 4
    KV_RING = 2
    HEAD_LOOPS = H // HEAD_RING
    assert S == P and H * HEAD_DIM == P and L == DM and HALVES == 2 and KVW == 512
    assert 2 * CAP == TPP * P and TPP == 5 and CH == 8
    TSLOT = 3 * P
    SKIP_B = 2 * P
    OFF_B = CAP - SKIP_B

    ROW = P + L
    skewed = nc.dram_tensor("skewed_kernels", (H, P * (ROW + 1)), F32, kind="Internal").ap()
    tokens_dram = nc.dram_tensor("tokens_dram", (T, DM), F32, kind="Internal").ap()
    picks_dram = nc.dram_tensor("picks_dram", (TOP_K * T, DM), F32, kind="Internal").ap()

    with ExitStack() as stack:
        def sb(name, shape, dt=F32):
            return stack.enter_context(nc.sbuf_tensor(name, shape, dt))

        def ps(name, shape, dt=F32):
            return stack.enter_context(nc.psum_tensor(name, shape, dt))

        def sem(name):
            return stack.enter_context(nc.semaphore(name))

        x_sb = sb("x_sb", [P, B, DM])
        ctx_sb = sb("ctx_sb", [P, B, DM])
        xn_sb = sb("xn_sb", [P, B, DM])
        ctxT = sb("ctxT", [P, HALVES, B, P])
        qT = sb("qT", [P, HALVES, B, P])
        attnT = sb("attnT", [P, HALVES, B, P])
        kern_sb = sb("kern_sb", [H, P + L])
        D_sb = sb("D_sb", [H, 1])
        toep = [sb(f"toep{i}", [P, L]) for i in range(HEAD_RING)]
        kv_space = sb("kv_space", [P, KV_RING * HALVES * KVW])
        kv = [kv_space[:, i * HALVES * KVW:(i + 1) * HALVES * KVW].rearrange("p (k c) -> p k c", k=HALVES)
              for i in range(KV_RING)]
        prod = [sb(f"prod{i}", [P, KVW]) for i in range(2)]
        xnT = [sb(f"xnT{i}", [P, HALVES, P]) for i in range(2)]
        ident = sb("ident", [P, P])
        gate_sb = sb("gate_sb", [P, HALVES, E])
        bias_rows = sb("bias_rows", [E * (CH + HALVES), P])
        biasT = sb("biasT", [P, E * (CH + HALVES)])
        gates2 = sb("gates2", [P, 2])
        tanh2 = sb("tanh2", [P, 2])
        stats = sb("stats", [P, B, 6])
        moments = sb("moments", [P, B, 2])
        rstd = sb("rstd", [P, B])
        minus_half = sb("minus_half", [P, B])
        NR = TOP_K * B
        expert_iota = sb("expert_iota", [P, E])
        tile_iota = sb("tile_iota", [P, TILES])
        col_iota = sb("col_iota", [P, P], F16)
        item_id = sb("item_id", [P, TOP_K, B])
        before = sb("before", [P, P], BF16)
        ones = sb("ones", [P, P], BF16)
        logits = sb("logits", [P, B, E])
        small = sb("small", [P, 4, B])
        probs = sb("probs", [P, B, E])
        top8 = sb("top8", [P, B, 8])
        top8_at = sb("top8_at", [P, B, 8], U32)
        chosen = sb("chosen", [P, TOP_K, B])
        onehot = sb("onehot", [P, TOP_K, B, E])
        taken = sb("taken", [P, B, E], BF16)
        before_me = sb("before_me", [P, TOP_K, B, E])
        position = sb("position", [P, TOP_K, B])
        dropped = sb("dropped", [P, TOP_K, B])
        slot = sb("slot", [P, TOP_K, B])
        slot_i = sb("slot_i", [P, TOP_K, B], I32)
        slot_tile_i = sb("slot_tile_i", [P, TOP_K, B], I32)
        slot_col_i = sb("slot_col_i", [P, TOP_K, B], I32)
        slot_tile = sb("slot_tile", [P, TOP_K, B])
        slot_col = sb("slot_col", [P, TOP_K, B])
        weight = sb("weight", [P, TOP_K, B])
        tile_hot = sb("tile_hot", [P, NR, TILES])
        tile_ids = sb("tile_ids", [P, NR, TILES], F16)
        col_hot = sb("col_hot", [P, NR, P], F16)
        table = sb("table", [P, TILES])
        table_a = sb("table_a", [P, TILES])
        table_b = sb("table_b", [P, TILES])
        table_c = sb("table_c", [P, TILES])
        table_d = sb("table_d", [P, TILES])
        source_row = sb("source_row", [P, TILES], U32)
        target_row = sb("target_row", [P, TILES], U32)
        w_raw = [[sb(f"w{m}_raw{a}", [P, HALVES * HID]) for m in (1, 2)] for a in range(2)]
        w_hi = [[sb(f"w{m}_hi{a}", [P, HALVES * HID], F32R) for m in (1, 2)] for a in range(2)]
        w_lo = [[sb(f"w{m}_lo{a}", [P, HALVES * HID], F32R) for m in (1, 2)] for a in range(2)]
        gathered = sb("gathered", [P, TPP, DM])
        in_hi = [sb(f"in_hi{a}", [P, HALVES, CAP], F32R) for a in range(2)]
        in_lo = [sb(f"in_lo{a}", [P, HALVES, CAP], F32R) for a in range(2)]
        hid = [sb(f"hid{i}", [P, CAP]) for i in range(2)]
        HR = 4
        hid_hi = [sb(f"hid_hi{i}", [P, CAP], F32R) for i in range(HR)]
        hid_lo = [sb(f"hid_lo{i}", [P, CAP], F32R) for i in range(HR)]
        outT = qT[:].rearrange("p k b c -> p (k b c)")[:, 0:HALVES * 2 * CAP].rearrange("p (k s) -> p k s", k=HALVES)
        rows = kv_space[:, 0:TPP * DM].rearrange("p (t d) -> p t d", t=TPP)
        zeros = sb("zeros", [P, DM])
        picks = [ctx_sb[:], attnT[:].rearrange("p k b c -> p (k b c)").rearrange("p (b d) -> p b d", b=B)]

        bank = [ps(f"bank{i}", [P, 512]) for i in range(8)]
        conv_bank = bank[0:4]
        turn_bank = bank[4:6]
        misc_bank = bank[6]
        pos_bank = bank[7]
        up_bank = bank[0:2]
        down_bank = [bank[2:4], bank[4:6]]
        back_bank = bank[6]
        turn_in = bank[7]

        kern_loaded = sem("kern_loaded")
        ctx_loaded = sem("ctx_loaded")
        x_loaded = sem("x_loaded")
        consts_loaded = sem("consts_loaded")
        kern_padded = sem("kern_padded")
        kern_in_dram = [sem(f"kern_in_dram{j}") for j in range(HEAD_LOOPS)]
        toep_loaded = [sem(f"toep_loaded{i}") for i in range(HEAD_RING)]
        w_loaded = [[sem(f"w{m}_loaded{a}") for m in (1, 2)] for a in range(2)]
        consts_made = sem("consts_made")
        dve_step = sem("dve_step")
        pool_step = sem("pool_step")
        act_step = sem("act_step")
        turned = sem("turned")
        turn_out = sem("turn_out")
        variance_ready = sem("variance_ready")
        rstd_ready = sem("rstd_ready")
        q_ready = sem("q_ready")
        kv_ready = sem("kv_ready")
        kv_used = sem("kv_used")
        conv_ready = sem("conv_ready")
        conv_used = sem("conv_used")
        multiplied = sem("multiplied")
        summed = sem("summed")
        back_turned = sem("back_turned")
        x2_ready = sem("x2_ready")
        xn_ready = sem("xn_ready")
        xn_stored = sem("xn_stored")
        xn_turned = sem("xn_turned")
        xnT_ready = sem("xnT_ready")
        logit_tile = sem("logit_tile")
        tanh_ready = sem("tanh_ready")
        shifted = sem("shifted")
        exp_ready = sem("exp_ready")
        taken_ready = sem("taken_ready")
        positions_ready = sem("positions_ready")
        hots_ready = sem("hots_ready")
        table_ready = sem("table_ready")
        rows_known = sem("rows_known")
        gather_a = sem("gather_a")
        gather_b = sem("gather_b")
        in_turned = sem("in_turned")
        in_hi_ready = sem("in_hi_ready")
        in_lo_ready = sem("in_lo_ready")
        w_hi_ready = sem("w_hi_ready")
        w1_lo_ready = sem("w1_lo_ready")
        w2_lo_ready = sem("w2_lo_ready")
        up_done = sem("up_done")
        down_done = sem("down_done")
        hid_ready = sem("hid_ready")
        hid_hi_ready = sem("hid_hi_ready")
        hid_lo_ready = sem("hid_lo_ready")
        outT_ready = sem("outT_ready")
        out_turned = sem("out_turned")
        row_ready = sem("row_ready")
        scattered = sem("scattered")
        zeroed = sem("zeroed")
        picks_zeroed = sem("picks_zeroed")
        picks_loaded = [sem(f"picks_loaded{k}") for k in range(TOP_K)]
        result_ready = sem("result_ready")
        stored = sem("stored")

        PIECES = 4
        PW = HALVES * HID // PIECES

        def w1_block(t, k, c):
            return t[:, k * HID + c * P:k * HID + (c + 1) * P]

        def w2_block(t, c, m):
            return t[:, c * DM + m * P:c * DM + (m + 1) * P]

        block = stack.enter_context(nc.Block())

        @block.sync
        def _(sp):
            sp.dma_start(kern_sb[:, P:P + L], ssm_kernel).then_inc(kern_loaded, 16)
            sp.dma_start(D_sb[:], D_skip.rearrange("(h a) -> h a", a=1)).then_inc(kern_loaded, 16)
            sp.dma_start(ctx_sb[:], ctx.rearrange("b s d -> s b d")).then_inc(ctx_loaded, 16)
            sp.dma_start(x_sb[:], x.rearrange("b s d -> s b d")).then_inc(x_loaded, 16)
            sp.wait_ge(kern_padded, 1)
            for j in range(HEAD_LOOPS):
                heads = slice(HEAD_RING * j, HEAD_RING * (j + 1))
                dst = bass.AP(skewed.tensor, HEAD_RING * j * P * (ROW + 1),
                              [[P * (ROW + 1), HEAD_RING], [ROW + 1, P], [1, ROW]])
                sp.dma_start(dst, kern_sb[heads, :].unsqueeze(1).broadcast_to([HEAD_RING, P, ROW])
                             ).then_inc(kern_in_dram[j], 16)

            def load_toeplitz(j, ring):
                for i in range(HEAD_RING):
                    if ring:
                        sp.wait_ge(kv_used, HEAD_RING * (j - 1) + i + 1)
                    src = skewed[bass.ds(HEAD_RING * j + i, 1), 0:P * ROW].rearrange("a (m l) -> (a m) l", m=P)
                    sp.dma_start(toep[i][:], src[:, P:P + L]).then_inc(toep_loaded[i], 16)

            sp.wait_ge(kern_in_dram[0], 16)
            load_toeplitz(0, False)
            sp.dma_start(gate_sb[:], gating_w.rearrange("(k p) e -> p k e", p=P)).then_inc(consts_loaded, 16)
            sp.dma_start(bias_rows[0:E * CH, :], b1.rearrange("e (c p) -> (e c) p", p=P)).then_inc(consts_loaded, 16)
            sp.dma_start(bias_rows[E * CH:, :], b2.rearrange("e (c p) -> (e c) p", p=P)).then_inc(consts_loaded, 16)
            sp.dma_start(gates2[:, 0:1], g_xattn.rearrange("(a b) -> a b", a=1).broadcast_to([P, 1])
                         ).then_inc(consts_loaded, 16)
            sp.dma_start(gates2[:, 1:2], g_ffn.rearrange("(a b) -> a b", a=1).broadcast_to([P, 1])
                         ).then_inc(consts_loaded, 16)

            def load_weights(g, a):
                n = 2 * g + a
                sp.dma_start(w_raw[a][0][:].rearrange("p (k h) -> p k h", k=HALVES),
                             w1[bass.ds(n, 1)].rearrange("e (k p) h -> p (e k) h", p=P)
                             ).then_inc(w_loaded[a][0], 16)
                sp.dma_start(w_raw[a][1][:].rearrange("p (c d) -> p c d", c=CH),
                             w2[bass.ds(n, 1)].rearrange("e (c p) d -> p (e c) d", p=P)
                             ).then_inc(w_loaded[a][1], 16)

            load_weights(0, 0)
            load_weights(0, 1)
            for j in range(1, HEAD_LOOPS):
                sp.wait_ge(kern_in_dram[j], 16)
            with sp.Fori(1, HEAD_LOOPS) as j:
                load_toeplitz(j, True)
            sp.wait_ge(zeroed, 1)
            for k in range(TOP_K):
                sp.dma_start(picks_dram[k * T:(k + 1) * T].rearrange("(b s) d -> s b d", s=S),
                             zeros[:].unsqueeze(1).broadcast_to([P, B, DM])
                             ).then_inc(picks_zeroed, 16)
            for b in range(B):
                sp.wait_ge(xn_ready, b + 1)
                sp.dma_start(tokens_dram[b * S:(b + 1) * S, :], xn_sb[:, b, :]).then_inc(xn_stored, 16)
            with sp.Fori(1, PAIRS) as g:
                for a in range(2):
                    sp.wait_ge(w1_lo_ready, PIECES * (2 * g + a - 1))
                    sp.wait_ge(w2_lo_ready, PIECES * (2 * g + a - 1))
                    load_weights(g, a)
            sp.wait_ge(scattered, 16 * TILES)
            for k in range(TOP_K):
                sp.dma_start(picks[k], picks_dram[k * T:(k + 1) * T].rearrange("(b s) d -> s b d", s=S)
                             ).then_inc(picks_loaded[k], 16)
            for b in range(B):
                sp.wait_ge(result_ready, b + 1)
                sp.dma_start(out[b], xn_sb[:, b, :]).then_inc(stored, 16)
            sp.wait_ge(stored, 16 * B)

        @block.gpsimd
        def _(pool):
            nc.gpsimd.memset(ident[:], 0.0).then_inc(pool_step, 1)
            nc.gpsimd.memset(ones[:], 1.0).then_inc(pool_step, 1)
            pool.wait_ge(pool_step, 2)
            nc.gpsimd.affine_select(out=ident[:], in_=ident[:], pattern=[[-1, P]], compare_op=ALU.not_equal,
                                    fill=1.0, base=0, channel_multiplier=1).then_inc(consts_made, 1)
            nc.gpsimd.affine_select(out=before[:], in_=ones[:], pattern=[[1, P]], compare_op=ALU.is_gt,
                                    fill=0.0, base=0, channel_multiplier=-1).then_inc(consts_made, 1)
            nc.gpsimd.iota(expert_iota[:], [[1, E]], base=0, channel_multiplier=0,
                           allow_small_or_imprecise_dtypes=True).then_inc(consts_made, 1)
            nc.gpsimd.iota(tile_iota[:], [[1, TILES]], base=0, channel_multiplier=0,
                           allow_small_or_imprecise_dtypes=True).then_inc(consts_made, 1)
            nc.gpsimd.iota(col_iota[:], [[1, P]], base=0, channel_multiplier=0,
                           allow_small_or_imprecise_dtypes=True).then_inc(consts_made, 1)
            nc.gpsimd.iota(item_id[:], [[T, TOP_K], [S, B]], base=1, channel_multiplier=1,
                           allow_small_or_imprecise_dtypes=True).then_inc(consts_made, 1)
            nc.gpsimd.memset(minus_half[:], -0.5).then_inc(pool_step, 1)
            nc.gpsimd.memset(zeros[:], 0.0).then_inc(zeroed, 1)

            def make_kv(j, first):
                for i in range(HEAD_RING):
                    h = HEAD_RING * j + i
                    if not first or i >= KV_RING:
                        pool.wait_ge(kv_used, h - KV_RING + 1)
                    for half in range(HALVES):
                        c = ctxT[:, half, :, bass.ds(HEAD_DIM * h, HEAD_DIM)]
                        shape = [P, B, HEAD_DIM, HEAD_DIM]
                        nc.gpsimd.tensor_tensor(
                            kv[i % KV_RING][:, half, :].rearrange("p (b j i) -> p b j i", b=B, j=HEAD_DIM),
                            c.unsqueeze(3).broadcast_to(shape), c.unsqueeze(2).broadcast_to(shape),
                            ALU.mult).then_inc(kv_ready, 1)

            def inverse_deviation(count):
                pool.wait_ge(variance_ready, count)
                nc.gpsimd.tensor_tensor(rstd[:], rstd[:], minus_half[:], ALU.pow).then_inc(rstd_ready, 1)

            pool.wait_ge(pool_step, 3)
            inverse_deviation(1)
            pool.wait_ge(turn_out, 4)
            make_kv(0, True)
            with pool.Fori(1, HEAD_LOOPS) as j:
                make_kv(j, False)

            def w2_split(n, a):
                for q in range(PIECES):
                    pool.wait_ge(w_hi_ready, 2 * PIECES * n + PIECES + q + 1)
                    cols = slice(q * PW, (q + 1) * PW)
                    nc.gpsimd.tensor_tensor(w_lo[a][1][:, cols], w_raw[a][1][:, cols],
                                            w_hi[a][1][:, cols].bitcast(F32), ALU.subtract
                                            ).then_inc(w2_lo_ready, 1)

            last_token = nc.gpsimd.to_reg(T - 1)
            last_pick = nc.gpsimd.to_reg(TOP_K * T - 1)

            def gather(g):
                for t in range(TPP):
                    nc.gpsimd.indirect_dma_start(
                        gathered[:, t, :], None, tokens_dram,
                        bass.IndirectOffsetOnAxis(ap=source_row[:, TPP * g + t:TPP * g + t + 1], axis=0),
                        bounds_check=last_token, oob_is_err=False).then_inc(gather_a if t < 3 else gather_b, 16)

            def scatter(g, t):
                pool.wait_ge(row_ready, TPP * g + t + 1)
                nc.gpsimd.indirect_dma_start(
                    picks_dram, bass.IndirectOffsetOnAxis(ap=target_row[:, TPP * g + t:TPP * g + t + 1], axis=0),
                    rows[:, t, :], None,
                    bounds_check=last_pick, oob_is_err=False).then_inc(scattered, 16)

            w2_split(0, 0)
            inverse_deviation(2)
            pool.wait_ge(xn_stored, 16 * B)
            pool.wait_ge(rows_known, 2)
            gather(0)
            pool.wait_ge(picks_zeroed, 16 * TOP_K)
            for g in range(PAIRS):
                w2_split(2 * g + 1, 1)
                if g > 0:
                    for t in range(2, TPP):
                        scatter(g - 1, t)
                if g < PAIRS - 1:
                    pool.wait_ge(in_turned, HALVES * (2 * g + 2))
                    gather(g + 1)
                    w2_split(2 * g + 2, 0)
                for t in range(2):
                    scatter(g, t)
            for t in range(2, TPP):
                scatter(PAIRS - 1, t)

        @block.tensor
        def _(pe):
            def turn(use, src, half, b0):
                wait_for(pe, turn_out, use - 1)
                for q in range(4):
                    b = b0 + q
                    last = pe.transpose(turn_bank[use % 2][:, q * P:(q + 1) * P],
                                        src[:, b, half * P:(half + 1) * P], ident[:])
                last.then_inc(turned, 1)

            pe.wait_ge(consts_made, 1)
            pe.wait_ge(ctx_loaded, 16)
            use = 0
            for half in range(HALVES):
                for b0 in (0, 4):
                    turn(use, ctx_sb, half, b0)
                    use += 1
            for half in range(HALVES):
                for b0 in (0, 4):
                    pe.wait_ge(q_ready, B)
                    turn(use, xn_sb, half, b0)
                    use += 1
            pe.wait_ge(consts_loaded, 16 * 5)
            NB = E * (CH + HALVES)
            pe.transpose(misc_bank[:, 0:NB], bias_rows[:], ident[0:NB, 0:NB]).then_inc(turned, 1)

            def convolve(j, first):
                for i in range(HEAD_RING):
                    h = HEAD_RING * j + i
                    pe.wait_ge(toep_loaded[i], 16 * (j + 1))
                    pe.wait_ge(kv_ready, HALVES * (h + 1))
                    y0, y1 = conv_bank[2 * (i % 2)], conv_bank[2 * (i % 2) + 1]
                    k = kv[i % KV_RING]
                    if not first or i >= 2:
                        pe.wait_ge(conv_used, HALVES * (h - 1))
                    pe.matmul(y0[:], toep[i][:, 0:P], k[:, 0, :], start=True, stop=True).then_inc(conv_ready, 1)
                    pe.matmul(y1[:], toep[i][:, P:L], k[:, 0, :], start=True, stop=False)
                    pe.matmul(y1[:], toep[i][:, 0:P], k[:, 1, :], start=False, stop=True).then_inc(kv_used, 1)

            convolve(0, True)
            with pe.Fori(1, HEAD_LOOPS) as j:
                convolve(j, False)

            pe.wait_ge(summed, HALVES * H)
            for b in range(B):
                for half in range(HALVES):
                    last = pe.transpose(conv_bank[b // 2][:, (b % 2) * DM + half * P:(b % 2) * DM + (half + 1) * P],
                                        attnT[:, half, b, :], ident[:])
                last.then_inc(back_turned, 1)

            def gate_tile(b):
                pe.wait_ge(xnT_ready, b + 1)
                for half in range(HALVES):
                    last = pe.matmul(pos_bank[:, 256 + b * E:256 + (b + 1) * E], xnT[b % 2][:, half, :],
                                     gate_sb[:, half, :], start=(half == 0), stop=(half == HALVES - 1))
                last.then_inc(logit_tile, 1)

            for b in range(B):
                pe.wait_ge(xn_ready, b + 1)
                if b == 0:
                    pe.wait_ge(turn_out, 8)
                if b >= 2:
                    pe.wait_ge(xnT_ready, b - 1)
                for half in range(HALVES):
                    last = pe.transpose(turn_bank[b % 2][:, half * P:(half + 1) * P],
                                        xn_sb[:, b, half * P:(half + 1) * P], ident[:])
                last.then_inc(xn_turned, 1)
                if b >= 1:
                    gate_tile(b - 1)
            gate_tile(B - 1)

            pe.wait_ge(taken_ready, 1)
            flat = taken[:].rearrange("p b e -> p (b e)")
            for b in range(B - 1):
                pe.matmul(pos_bank[:, (b + 1) * E:B * E], ones[:],
                          taken[:, b:b + 1, :].broadcast_to([P, B - 1 - b, E]),
                          start=(b == 0), stop=False, skip_group_check=True)
            pe.matmul(pos_bank[:, 0:B * E], before[:], flat, start=False, stop=True, skip_group_check=True
                      ).then_inc(positions_ready, 1)
            pe.wait_ge(hots_ready, NR + 1)
            for r in range(NR):
                last = pe.matmul(misc_bank[:, 128:128 + TILES], col_hot[:, r, :], tile_ids[:, r, :],
                                 start=(r == 0), stop=(r == NR - 1))
            last.then_inc(table_ready, 1)

            def inputs(g, a, half):
                if half == 0:
                    pe.wait_ge(gather_a, 16 * 3 * (g + 1))
                    if a == 1:
                        pe.wait_ge(gather_b, 16 * 2 * (g + 1))
                n2 = 2 * (2 * g + a) + half
                wait_for(pe, in_lo_ready, n2)
                t0 = 0 if a == 0 else 2
                for t in range(3):
                    last = pe.transpose(turn_in[:, t * P:(t + 1) * P],
                                        gathered[:, t0 + t, half * P:(half + 1) * P], ident[:])
                last.then_inc(in_turned, 1)

            def up(n, a, c):
                if c == 0:
                    pe.wait_ge(in_lo_ready, HALVES * (n + 1))
                    pe.wait_ge(w_hi_ready, 2 * PIECES * n + PIECES)
                    pe.wait_ge(w1_lo_ready, PIECES * (n + 1))
                wait_for(pe, hid_ready, CH * n + c - 1)
                bankc = up_bank[c % 2][:, 0:CAP]
                for k in range(HALVES):
                    hi, lo = w1_block(w_hi[a][0], k, c), w1_block(w_lo[a][0], k, c)
                    pe.matmul(bankc, hi, in_hi[a][:, k, :], start=(k == 0), stop=False)
                    pe.matmul(bankc, hi, in_lo[a][:, k, :], start=False, stop=False)
                    last = pe.matmul(bankc, lo, in_hi[a][:, k, :], start=False, stop=(k == HALVES - 1))
                last.then_inc(up_done, 1)

            def down(n, a, c):
                if c == 0:
                    pe.wait_ge(w_hi_ready, 2 * PIECES * (n + 1))
                    pe.wait_ge(w2_lo_ready, PIECES * (n + 1))
                    wait_for(pe, outT_ready, n - 1)
                pe.wait_ge(hid_lo_ready, CH * n + c + 1)
                for m in range(HALVES):
                    hi, lo = w2_block(w_hi[a][1], c, m), w2_block(w_lo[a][1], c, m)
                    bankm = down_bank[a][m][:, 0:CAP]
                    pe.matmul(bankm, hi, hid_hi[c % HR][:], start=(c == 0), stop=False)
                    pe.matmul(bankm, hi, hid_lo[c % HR][:], start=False, stop=False)
                    last = pe.matmul(bankm, lo, hid_hi[c % HR][:], start=False, stop=(c == CH - 1))
                last.then_inc(down_done, 1)

            def back(g, t):
                if t == 0:
                    pe.wait_ge(outT_ready, 2 * g + 1)
                if t == 2:
                    pe.wait_ge(outT_ready, 2 * g + 2)
                wait_for(pe, row_ready, TPP * g + t)
                for half in range(HALVES):
                    last = pe.transpose(back_bank[:, half * P:(half + 1) * P],
                                        outT[:, half, t * P:(t + 1) * P], ident[:])
                last.then_inc(out_turned, 1)

            def pair(g, first, last):
                for a in range(2):
                    n = 2 * g + a
                    for c in range(CH):
                        up(n, a, c)
                        if c >= 2:
                            down(n, a, c - 2)
                        elif a == 1 or not first:
                            down(n - 1, 1 - a, c + CH - 2)
                        if a == 0 and not first and 3 <= c < 6:
                            back(g - 1, c - 1)
                        if a == 1 and 3 <= c < 5:
                            back(g, c - 3)
                        if 4 <= c < 6 and a == 0:
                            inputs(g, 1, c - 4)
                        if 4 <= c < 6 and a == 1 and not last:
                            inputs(g + 1, 0, c - 4)

            pe.wait_ge(rows_known, 2)
            inputs(0, 0, 0)
            inputs(0, 0, 1)
            pair(0, True, False)
            with pe.Fori(1, PAIRS - 1) as g:
                pair(g, False, False)
            pair(PAIRS - 1, False, True)
            down(E - 1, 1, CH - 2)
            down(E - 1, 1, CH - 1)
            for t in range(2, TPP):
                back(PAIRS - 1, t)

        @block.scalar
        def _(act):
            act.wait_ge(consts_loaded, 16 * 5)
            nc.scalar.activation(tanh2[:], gates2[:], ACT.Tanh).then_inc(tanh_ready, 1)
            for use in range(8):
                dst = ctxT if use < 4 else qT
                half, b0 = (use % 4) // 2, 4 * (use % 2)
                act.wait_ge(turned, use + 1)
                nc.scalar.copy(dst[:, half, b0:b0 + 4, :].rearrange("p b c -> p (b c)"),
                               turn_bank[use % 2][:]).then_inc(turn_out, 1)
            act.wait_ge(turned, 9)
            nc.scalar.copy(biasT[:], misc_bank[:, 0:E * (CH + HALVES)]).then_inc(act_step, 1)

            def split(g, a, piece):
                m, q = piece // PIECES, piece % PIECES
                n = 2 * g + a
                if q == 0:
                    act.wait_ge(w_loaded[a][m], 16 * (g + 1))
                    if m == 0:
                        wait_for(act, up_done, CH * (n - 1))
                    else:
                        wait_for(act, down_done, CH * (n - 1))
                cols = slice(q * PW, (q + 1) * PW)
                nc.scalar.copy(w_hi[a][m][:, cols], w_raw[a][m][:, cols]).then_inc(w_hi_ready, 1)

            def input_high(g, a, half):
                n2 = 2 * (2 * g + a) + half
                act.wait_ge(in_turned, n2 + 1)
                if half == 0:
                    wait_for(act, up_done, CH * (2 * g + a - 1))
                off = 0 if a == 0 else OFF_B
                nc.scalar.copy(in_hi[a][:, half, :], turn_in[:, off:off + CAP]).then_inc(in_hi_ready, 1)

            def hidden(n, c):
                act.wait_ge(up_done, CH * n + c + 1)
                wait_for(act, hid_lo_ready, CH * n + c - 1)
                nc.scalar.activation(hid[c % 2][:], up_bank[c % 2][:, 0:CAP], ACT.Relu,
                                     bias=biasT[:, bass.ds(CH * n + c, 1)]).then_inc(hid_ready, 1)

            def output(n, a, g):
                act.wait_ge(down_done, CH * (n + 1))
                wait_for(act, out_turned, TPP * g)
                for m in range(HALVES):
                    last = nc.scalar.activation(outT[:, m, a * CAP:(a + 1) * CAP], down_bank[a][m][:, 0:CAP],
                                                ACT.Identity, bias=biasT[:, bass.ds(E * CH + HALVES * n + m, 1)])
                last.then_inc(outT_ready, 1)

            for piece in range(2 * PIECES):
                split(0, 0, piece)
            for b in range(B):
                act.wait_ge(xn_turned, b + 1)
                if b >= 2:
                    act.wait_ge(logit_tile, b - 1)
                nc.scalar.copy(xnT[b % 2][:].rearrange("p k s -> p (k s)"), turn_bank[b % 2][:, 0:DM]
                               ).then_inc(xnT_ready, 1)
            act.wait_ge(shifted, 1)
            nc.scalar.activation(probs[:], logits[:], ACT.Exp).then_inc(exp_ready, 1)
            act.wait_ge(act_step, 1)
            input_high(0, 0, 0)
            input_high(0, 0, 1)

            def pair(g, first, last):
                for a in range(2):
                    n = 2 * g + a
                    for c in range(CH):
                        hidden(n, c)
                        if c == 1 and (a == 1 or not first):
                            output(n - 1, 1 - a, g if a == 1 else g - 1)
                        if c >= 1 and not (last and a == 1):
                            g2, a2 = (g, 1) if a == 0 else (g + 1, 0)
                            split(g2, a2, c - 1)
                            if c == CH - 1:
                                split(g2, a2, c)
                            if 4 <= c < 6:
                                input_high(g2, a2, c - 4)

            pair(0, True, False)
            with act.Fori(1, PAIRS - 1) as g:
                pair(g, False, False)
            pair(PAIRS - 1, False, True)
            output(E - 1, 1, PAIRS - 1)

        @block.vector
        def _(dve):
            steps = [0]

            def step(ins):
                steps[0] += 1
                ins.then_inc(dve_step, 1)
                dve.wait_ge(dve_step, steps[0])

            step(nc.vector.memset(kern_sb[:, 0:P], 0.0))
            dve.wait_ge(kern_loaded, 32)
            nc.vector.tensor_tensor(kern_sb[:, P:P + 1], kern_sb[:, P:P + 1], D_sb[:], ALU.add
                                    ).then_inc(kern_padded, 1)

            def normalize(ready, count):
                for b in range(B):
                    last = nc.vector.bn_stats(stats[:, b, :], x_sb[:, b, :])
                step(last)
                for b in range(B):
                    last = nc.vector.bn_aggr(moments[:, b, :], stats[:, b, :])
                step(last)
                nc.vector.tensor_scalar(rstd[:], moments[:, :, 1], LN_EPS, None, ALU.add).then_inc(variance_ready, 1)
                dve.wait_ge(rstd_ready, count)
                for b in range(B):
                    nc.vector.tensor_scalar(xn_sb[:, b, :], x_sb[:, b, :], moments[:, b, 0:1], rstd[:, b:b + 1],
                                            ALU.subtract, ALU.mult).then_inc(ready, 1)

            dve.wait_ge(x_loaded, 16)
            normalize(q_ready, 1)

            def add_up(j, first):
                for i in range(HEAD_RING):
                    h = HEAD_RING * j + i
                    for half in range(HALVES):
                        k = HALVES * i + half
                        done = HALVES * HEAD_RING * j + k
                        if half == 0:
                            dve.wait_ge(conv_ready, h + 1)
                        else:
                            dve.wait_ge(kv_used, h + 1)
                        if not first or k >= 2:
                            dve.wait_ge(summed, done - 1)
                        q = qT[:, half, :, bass.ds(HEAD_DIM * h, HEAD_DIM)]
                        nc.vector.tensor_tensor(
                            prod[k % 2][:].rearrange("p (b j i) -> p b j i", b=B, j=HEAD_DIM),
                            conv_bank[k % 4][:].rearrange("p (b j i) -> p b j i", b=B, j=HEAD_DIM),
                            q.unsqueeze(2).broadcast_to([P, B, HEAD_DIM, HEAD_DIM]), ALU.mult
                        ).then_inc(conv_used, 1)
                        dve.wait_ge(conv_used, done + 1)
                        nc.vector.tensor_reduce(
                            attnT[:, half, :, bass.ds(HEAD_DIM * h, HEAD_DIM)],
                            prod[k % 2][:].rearrange("p (b j i) -> p b j i", b=B, j=HEAD_DIM),
                            AX_X, ALU.add).then_inc(summed, 1)

            dve.wait_ge(turn_out, 8)
            add_up(0, True)
            with dve.Fori(1, HEAD_LOOPS) as j:
                add_up(j, False)

            dve.wait_ge(tanh_ready, 1)
            for b in range(B):
                dve.wait_ge(back_turned, 2 * (b // 2) + 2)
                last = nc.vector.scalar_tensor_tensor(
                    out=x_sb[:, b, :], in0=conv_bank[b // 2][:, (b % 2) * DM:(b % 2 + 1) * DM],
                    scalar=tanh2[:, 0:1], in1=x_sb[:, b, :], op0=ALU.mult, op1=ALU.add)
            step(last)
            normalize(xn_ready, 2)

            dve.wait_ge(logit_tile, B)
            lg = pos_bank[:, 256:256 + B * E].rearrange("p (b e) -> p b e", b=B)
            bc = [P, B, E]
            step(nc.vector.tensor_reduce(small[:, 0, :], lg, AX_X, ALU.max))
            nc.vector.tensor_tensor(logits[:], lg, small[:, 0, :].unsqueeze(2).broadcast_to(bc), ALU.subtract
                                    ).then_inc(shifted, 1)
            dve.wait_ge(exp_ready, 1)
            step(nc.vector.tensor_reduce(small[:, 1, :], probs[:], AX_X, ALU.add))
            step(nc.vector.reciprocal(small[:, 2, :], small[:, 1, :]))
            step(nc.vector.tensor_tensor(probs[:], probs[:], small[:, 2, :].unsqueeze(2).broadcast_to(bc), ALU.mult))
            for b in range(B):
                last = nc.vector.max(top8[:, b, :], probs[:, b, :])
            step(last)
            for b in range(B):
                last = nc.vector.max_index(top8_at[:, b, :], top8[:, b, :], probs[:, b, :])
            step(last)
            step(nc.vector.tensor_copy(chosen[:].rearrange("p k b -> p b k"), top8_at[:, :, 0:TOP_K]))
            dve.wait_ge(consts_made, 6)
            for k in range(TOP_K):
                last = nc.vector.tensor_tensor(onehot[:, k], chosen[:, k, :].unsqueeze(2).broadcast_to(bc),
                                               expert_iota[:].unsqueeze(1).broadcast_to(bc), ALU.is_equal)
            step(last)
            nc.vector.tensor_tensor(taken[:], onehot[:, 0], onehot[:, 1], ALU.add).then_inc(taken_ready, 1)
            dve.wait_ge(positions_ready, 1)
            pos = pos_bank[:, 0:B * E].rearrange("p (b e) -> p b e", b=B)
            for k in range(TOP_K):
                last = nc.vector.tensor_tensor(before_me[:, k], onehot[:, k], pos, ALU.mult)
            step(last)
            step(nc.vector.tensor_reduce(position[:], before_me[:], AX_X, ALU.add))
            step(nc.vector.tensor_scalar(dropped[:], position[:], float(CAP), OUT_OF_BOUNDS, ALU.is_ge, ALU.mult))
            step(nc.vector.scalar_tensor_tensor(out=slot[:], in0=chosen[:], scalar=float(CAP), in1=position[:],
                                                op0=ALU.mult, op1=ALU.add))
            step(nc.vector.tensor_tensor(slot[:], slot[:], dropped[:], ALU.add))
            step(nc.vector.tensor_copy(slot_i[:], slot[:]))
            nc.vector.tensor_scalar(slot_tile_i[:], slot_i[:], 7, None, ALU.logical_shift_right)
            step(nc.vector.tensor_scalar(slot_col_i[:], slot_i[:], P - 1, None, ALU.bitwise_and))
            nc.vector.tensor_copy(slot_tile[:], slot_tile_i[:])
            step(nc.vector.tensor_copy(slot_col[:], slot_col_i[:]))
            cols = slot_col[:].rearrange("p k b -> p (k b)")
            for r in range(NR):
                nc.vector.tensor_scalar(col_hot[:, r, :], col_iota[:], cols[:, r:r + 1], None, ALU.is_equal
                                        ).then_inc(hots_ready, 1)
            bt = [P, NR, TILES]
            step(nc.vector.tensor_tensor(tile_hot[:], slot_tile[:].rearrange("p k b -> p (k b)").unsqueeze(2).broadcast_to(bt),
                                         tile_iota[:].unsqueeze(1).broadcast_to(bt), ALU.is_equal))
            nc.vector.tensor_tensor(tile_ids[:], tile_hot[:],
                                    item_id[:].rearrange("p k b -> p (k b)").unsqueeze(2).broadcast_to(bt),
                                    ALU.mult).then_inc(hots_ready, 1)
            dve.wait_ge(table_ready, 1)
            step(nc.vector.tensor_copy(table[:], misc_bank[:, 128:128 + TILES]))
            nc.vector.tensor_scalar(table_a[:], table[:], float(T), -float(T), ALU.is_gt, ALU.mult)
            step(nc.vector.tensor_scalar(table_b[:], table[:], 1.0, -1.0, ALU.max, ALU.add))
            nc.vector.tensor_tensor(source_row[:], table_b[:], table_a[:], ALU.add).then_inc(rows_known, 1)
            step(nc.vector.tensor_scalar(table_c[:], table[:], 0.0, OUT_OF_BOUNDS, ALU.is_equal, ALU.mult))
            step(nc.vector.tensor_tensor(table_d[:], table_c[:], table[:], ALU.add))
            nc.vector.tensor_scalar(target_row[:], table_d[:], 1.0, None, ALU.subtract).then_inc(rows_known, 1)
            both = top8[:, :, 0:TOP_K].rearrange("p b k -> p k b")
            step(nc.vector.tensor_tensor(small[:, 3, :], both[:, 0, :], both[:, 1, :], ALU.add))
            step(nc.vector.tensor_scalar(small[:, 3, :], small[:, 3, :], NORM_EPS, None, ALU.add))
            step(nc.vector.reciprocal(small[:, 3, :], small[:, 3, :]))
            step(nc.vector.tensor_tensor(weight[:], both, small[:, 3, :].unsqueeze(1).broadcast_to([P, TOP_K, B]),
                                         ALU.mult))
            step(nc.vector.tensor_scalar(dropped[:], position[:], float(CAP), tanh2[:, 1:2], ALU.is_lt, ALU.mult))
            step(nc.vector.tensor_tensor(weight[:], weight[:], dropped[:], ALU.mult))

            def w1_split(g, a, q):
                n = 2 * g + a
                dve.wait_ge(w_hi_ready, 2 * PIECES * n + q + 1)
                cols = slice(q * PW, (q + 1) * PW)
                nc.vector.tensor_tensor(w_lo[a][0][:, cols], w_raw[a][0][:, cols],
                                        w_hi[a][0][:, cols].bitcast(F32), ALU.subtract).then_inc(w1_lo_ready, 1)

            def input_low(g, a, half):
                n2 = 2 * (2 * g + a) + half
                dve.wait_ge(in_hi_ready, n2 + 1)
                off = 0 if a == 0 else OFF_B
                nc.vector.tensor_tensor(in_lo[a][:, half, :], turn_in[:, off:off + CAP],
                                        in_hi[a][:, half, :].bitcast(F32), ALU.subtract).then_inc(in_lo_ready, 1)

            def hidden_split(n, c):
                dve.wait_ge(hid_ready, CH * n + c + 1)
                wait_for(dve, down_done, CH * n + c - HR + 1)
                nc.vector.tensor_copy(hid_hi[c % HR][:], hid[c % 2][:]).then_inc(hid_hi_ready, 1)
                dve.wait_ge(hid_hi_ready, CH * n + c + 1)
                nc.vector.tensor_tensor(hid_lo[c % HR][:], hid[c % 2][:], hid_hi[c % HR][:].bitcast(F32),
                                        ALU.subtract).then_inc(hid_lo_ready, 1)

            def row_tile(g, t):
                dve.wait_ge(out_turned, TPP * g + t + 1)
                if t == 0:
                    wait_for(dve, scattered, 16 * TPP * g)
                nc.vector.tensor_copy(rows[:, t, :], back_bank[:, 0:DM]).then_inc(row_ready, 1)

            for q in range(PIECES):
                w1_split(0, 0, q)
            input_low(0, 0, 0)
            input_low(0, 0, 1)

            def pair(g, first, last):
                for a in range(2):
                    n = 2 * g + a
                    for c in range(CH):
                        hidden_split(n, c)
                        if a == 0 and not first and 3 <= c < 6:
                            row_tile(g - 1, c - 1)
                        if a == 1 and 3 <= c < 5:
                            row_tile(g, c - 3)
                        if c >= 1 and not (last and a == 1):
                            g2, a2 = (g, 1) if a == 0 else (g + 1, 0)
                            if c <= PIECES:
                                w1_split(g2, a2, c - 1)
                            if 4 <= c < 6:
                                input_low(g2, a2, c - 4)

            pair(0, True, False)
            with dve.Fori(1, PAIRS - 1) as g:
                pair(g, False, False)
            pair(PAIRS - 1, False, True)
            for t in range(2, TPP):
                row_tile(PAIRS - 1, t)

            dve.wait_ge(picks_loaded[0], 16)
            for b in range(B):
                last = nc.vector.scalar_tensor_tensor(out=x_sb[:, b, :], in0=picks[0][:, b, :],
                                                      scalar=weight[:, 0, b:b + 1], in1=x_sb[:, b, :],
                                                      op0=ALU.mult, op1=ALU.add)
            step(last)
            dve.wait_ge(picks_loaded[1], 16)
            for b in range(B):
                nc.vector.scalar_tensor_tensor(out=xn_sb[:, b, :], in0=picks[1][:, b, :],
                                               scalar=weight[:, 1, b:b + 1], in1=x_sb[:, b, :],
                                               op0=ALU.mult, op1=ALU.add).then_inc(result_ready, 1)


_INS = ['x', 'ctx_2048', 'g_xattn', 'g_ffn', 'L0_xattn_ssm_kernel', 'L0_xattn_D', 'L0_ffn_gating_w',
        'L0_ffn_w1', 'L0_ffn_b1', 'L0_ffn_w2', 'L0_ffn_b2']


def kernel(**inputs):
    import numpy as np
    import concourse.bacc as bacc
    from concourse.bass_utils import run_bass_kernel_spmd

    nc = bacc.Bacc("TRN2", target_bir_lowering=False, num_devices=1)
    arrays, args = {}, []
    for name in _INS:
        a = np.ascontiguousarray(inputs[name])
        arrays[f"in_{name}"] = a
        args.append(nc.dram_tensor(f"in_{name}", a.shape, mybir.dt.from_np(a.dtype), kind="ExternalInput").ap())
    out = nc.dram_tensor("out", arrays["in_x"].shape, F32, kind="ExternalOutput").ap()
    build_gated_block(nc, *args, out)
    result = run_bass_kernel_spmd(nc, [arrays], core_ids=[0])
    return result.results[0]["out"]
```

```python
from contextlib import ExitStack

import concourse.bass as bass
from concourse import mybir

F32 = mybir.dt.float32
F32R = mybir.dt.float32r
F16 = mybir.dt.float16
BF16 = mybir.dt.bfloat16
I32 = mybir.dt.int32
U32 = mybir.dt.uint32
ALU = mybir.AluOpType
ACT = mybir.ActivationFunctionType
AX_X = mybir.AxisListType.X

P = 128
HEAD_DIM = 8
TOP_K = 2
LN_EPS = 1e-5
NORM_EPS = 1e-8
OUT_OF_BOUNDS = 8192.0


def wait_for(engine, semaphore, value):
    if not isinstance(value, int) or value > 0:
        engine.wait_ge(semaphore, value)


def build_gated_block(nc, x, ctx, g_xattn, g_ffn, ssm_kernel, D_skip, gating_w, w1, b1, w2, b2, out):
    B, S, DM = x.shape
    H, L = ssm_kernel.shape
    E, _, HID = w1.shape
    HALVES = DM // P
    T = B * S
    CAP = -(-T * TOP_K * 5 // (E * 4))
    SLOTS = E * CAP
    TILES = SLOTS // P
    PAIRS = E // 2
    TPP = TILES // PAIRS
    CH = HID // P
    KVW = B * HEAD_DIM * HEAD_DIM
    HEAD_RING = 4
    KV_RING = 4
    SKEW = 2
    PROD_RING = 8
    SUM_LAG = 2
    HB = HEAD_DIM // 2
    HEAD_LOOPS = H // HEAD_RING
    GB = B // 2
    ENDS = 4
    EB = B // ENDS
    assert S == P and H * HEAD_DIM == P and L == DM and HALVES == 2 and KVW == 512
    assert 2 * CAP == TPP * P and TPP == 5 and CH == 8

    ROW = P + L
    skewed = nc.dram_tensor("skewed_kernels", (H, P * (ROW + 1)), F32, kind="Internal").ap()
    tokens_dram = nc.dram_tensor("tokens_dram", (T, DM), F32, kind="Internal").ap()
    picks_dram = nc.dram_tensor("picks_dram", (TOP_K * T, DM), F32, kind="Internal").ap()

    with ExitStack() as stack:
        def sb(name, shape, dt=F32):
            return stack.enter_context(nc.sbuf_tensor(name, shape, dt))

        def ps(name, shape, dt=F32):
            return stack.enter_context(nc.psum_tensor(name, shape, dt))

        def sem(name):
            return stack.enter_context(nc.semaphore(name))

        x_sb = sb("x_sb", [P, B, DM])
        ctx_sb = sb("ctx_sb", [P, B, DM])
        xn_sb = sb("xn_sb", [P, B, DM])
        ctxT = sb("ctxT", [P, HALVES, B, P])
        qT = sb("qT", [P, HALVES, B, P])
        attnT = sb("attnT", [P, HALVES, B, P])
        kern_sb = sb("kern_sb", [H, P + L])
        D_sb = sb("D_sb", [H, 1])
        toep = [sb(f"toep{i}", [P, L]) for i in range(HEAD_RING)]
        kv_space = sb("kv_space", [P, 2 * HALVES * KVW])
        prod_space = sb("prod_space", [P, PROD_RING // 2 * KVW])
        ident = sb("ident", [P, P])
        gate_sb = sb("gate_sb", [P, HALVES, E])
        bias_rows = sb("bias_rows", [E * (CH + HALVES), P])
        biasT = sb("biasT", [P, E * (CH + HALVES)])
        gates2 = sb("gates2", [P, 2])
        tanh2 = sb("tanh2", [P, 2])
        stats = sb("stats", [P, B, 6])
        moments = sb("moments", [P, B, 2])
        rstd = sb("rstd", [P, B])
        minus_half = sb("minus_half", [P, B])
        neg_mean = sb("neg_mean", [P, B])
        shift = sb("shift", [P, B])
        deviation = sb("deviation", [P, B])
        gate_c = sb("gate_c", [P, HALVES, E])
        scaled_gate = sb("scaled_gate", [P, HALVES, E])
        NR = TOP_K * B
        POOL_HOTS = 4
        expert_iota = sb("expert_iota", [P, E])
        tile_iota = sb("tile_iota", [P, TILES])
        col_iota = sb("col_iota", [P, P], F16)
        item_id = sb("item_id", [P, B, TOP_K])
        before = sb("before", [P, P], BF16)
        ones = sb("ones", [P, P], BF16)
        logits = sb("logits", [P, B, E])
        small = sb("small", [P, 4, B])
        probs = sb("probs", [P, B, E])
        top8 = sb("top8", [P, B, 8])
        top8_at = sb("top8_at", [P, B, 8], U32)
        chosen = sb("chosen", [P, B, TOP_K])
        onehot = sb("onehot", [P, B, TOP_K, E])
        taken = sb("taken", [P, B, E], BF16)
        before_me = sb("before_me", [P, B, TOP_K, E])
        position = sb("position", [P, B, TOP_K])
        dropped = sb("dropped", [P, B, TOP_K])
        slot = sb("slot", [P, B, TOP_K])
        slot_i = sb("slot_i", [P, B, TOP_K], I32)
        slot_tile_i = sb("slot_tile_i", [P, B, TOP_K], I32)
        slot_col_i = sb("slot_col_i", [P, B, TOP_K], I32)
        slot_col = sb("slot_col", [P, B, TOP_K])
        weight = sb("weight", [P, B, TOP_K])
        tile_hot = sb("tile_hot", [P, NR, TILES])
        tile_ids = sb("tile_ids", [P, NR, TILES], F16)
        col_hot = sb("col_hot", [P, NR, P], F16)
        table_a = sb("table_a", [P, TILES])
        table_b = sb("table_b", [P, TILES])
        table_c = sb("table_c", [P, TILES])
        source_row = sb("source_row", [P, TILES], U32)
        target_row = sb("target_row", [P, TILES], U32)
        w_raw = [[sb(f"w{m}_raw{a}", [P, HALVES * HID]) for m in (1, 2)] for a in range(2)]
        w_hi = [[sb(f"w{m}_hi{a}", [P, HALVES * HID], F32R) for m in (1, 2)] for a in range(2)]
        w_lo = [[sb(f"w{m}_lo{a}", [P, HALVES * HID], F32R) for m in (1, 2)] for a in range(2)]
        def in_columns(t, width, n):
            return [t[:, i * width:(i + 1) * width] for i in range(n)]

        kv = [t.rearrange("p (k c) -> p k c", k=HALVES)
              for t in in_columns(kv_space[:], HALVES * KVW, 2) + in_columns(w_raw[1][0][:], HALVES * KVW, 2)]
        prod = (in_columns(prod_space[:], KVW, PROD_RING // 2)
                + in_columns(w_raw[1][1][:], KVW, PROD_RING // 2))
        gathered = ctxT[:].rearrange("p k b c -> p (k b c)")[:, 0:TPP * DM].rearrange("p (t d) -> p t d", t=TPP)
        in_hi = [sb(f"in_hi{a}", [P, HALVES, CAP], F32R) for a in range(2)]
        in_lo = [sb(f"in_lo{a}", [P, HALVES, CAP], F32R) for a in range(2)]
        hid = [sb(f"hid{i}", [P, CAP]) for i in range(2)]
        ones_f = hid[0][:, 0:P]
        scaled_ident = hid[1][:, 0:P]
        HR = 4
        hid_hi = [sb(f"hid_hi{i}", [P, CAP], F32R) for i in range(HR)]
        hid_lo = [sb(f"hid_lo{i}", [P, CAP], F32R) for i in range(HR)]
        outT = qT[:].rearrange("p k b c -> p (k b c)")[:, 0:HALVES * 2 * CAP].rearrange("p (k s) -> p k s", k=HALVES)
        rows = kv_space[:, 0:TPP * DM].rearrange("p (t d) -> p t d", t=TPP)
        zeros = sb("zeros", [P, DM])
        picks = [ctx_sb[:], attnT[:].rearrange("p k b c -> p (k b c)").rearrange("p (b d) -> p b d", b=B)]

        bank = [ps(f"bank{i}", [P, 512]) for i in range(8)]
        conv_bank = bank[0:4]
        turn_bank = [bank[4], bank[5], bank[2], bank[3]]
        x2_bank = [bank[6], bank[7], bank[4], bank[5]]
        gate_bank = bank[0]
        pos_bank = bank[1]
        up_bank = bank[0:2]
        down_bank = [bank[2:4], bank[4:6]]
        back_bank = bank[6]
        turn_in = bank[7]

        def by_pair(t):
            return t.rearrange("p (b j i) -> p b j i", b=B, j=HEAD_DIM)

        def queries(h, half):
            return qT[:, half, :, bass.ds(HEAD_DIM * h, HEAD_DIM)].unsqueeze(2).broadcast_to(
                [P, B, HEAD_DIM, HEAD_DIM])

        QUADS = [(slice(None), slice(None), slice(0, HB), slice(0, HEAD_DIM)),
                 (slice(None), slice(None), slice(HB, HEAD_DIM), slice(HB, HEAD_DIM))]

        POOL_ITEM = 3
        POOL_LAG = 2

        kern_loaded = sem("kern_loaded")
        ctx_loaded = [sem(f"ctx_loaded{q}") for q in range(2)]
        x_loaded = [sem(f"x_loaded{q}") for q in range(2)]
        consts_loaded = sem("consts_loaded")
        kern_padded = sem("kern_padded")
        kern_in_dram = [sem(f"kern_in_dram{j}") for j in range(H // SKEW)]
        toep_loaded = [sem(f"toep_loaded{i}") for i in range(HEAD_RING)]
        w_loaded = [[sem(f"w{m}_loaded{a}") for m in (1, 2)] for a in range(2)]
        consts_made = sem("consts_made")
        dve_step = sem("dve_step")
        pool_step = sem("pool_step")
        act_step = sem("act_step")
        turned = sem("turned")
        turn_out = sem("turn_out")
        variance_ready = sem("variance_ready")
        rstd_ready = sem("rstd_ready")
        shift_ready = sem("shift_ready")
        queries_gated = sem("queries_gated")
        gate_summed = sem("gate_summed")
        gate_centered = sem("gate_centered")
        old_logits_ready = sem("old_logits_ready")
        gate_scaled = sem("gate_scaled")
        q_ready = sem("q_ready")
        kv_ready = sem("kv_ready")
        kv_used = sem("kv_used")
        conv_ready = sem("conv_ready")
        conv_kept = sem("conv_kept")
        multiplied = sem("multiplied")
        pool_multiplied = sem("pool_multiplied")
        summed = sem("summed")
        x2_ready = sem("x2_ready")
        x2_kept = sem("x2_kept")
        xn_ready = [sem(f"xn_ready{q}") for q in range(2)]
        xn_stored = sem("xn_stored")
        gated = sem("gated")
        tanh_ready = sem("tanh_ready")
        shifted = sem("shifted")
        exp_ready = sem("exp_ready")
        taken_ready = sem("taken_ready")
        positions_ready = sem("positions_ready")
        slot_col_ready = sem("slot_col_ready")
        tiles_marked = sem("tiles_marked")
        dve_hots = sem("dve_hots")
        pool_hots = sem("pool_hots")
        table_ready = sem("table_ready")
        rows_known = sem("rows_known")
        gather_a = sem("gather_a")
        gather_b = sem("gather_b")
        in_turned = sem("in_turned")
        in_hi_ready = sem("in_hi_ready")
        in_lo_ready = sem("in_lo_ready")
        w_hi_ready = sem("w_hi_ready")
        w1_lo_ready = sem("w1_lo_ready")
        w2_lo_ready = sem("w2_lo_ready")
        up_done = sem("up_done")
        down_done = sem("down_done")
        hid_ready = sem("hid_ready")
        hid_hi_ready = sem("hid_hi_ready")
        hid_lo_ready = sem("hid_lo_ready")
        outT_ready = sem("outT_ready")
        out_turned = sem("out_turned")
        row_ready = sem("row_ready")
        scattered = sem("scattered")
        zeroed = sem("zeroed")
        picks_zeroed = sem("picks_zeroed")
        picks_loaded = [sem(f"picks_loaded{q}") for q in range(ENDS)]
        first_added = sem("first_added")
        result_ready = sem("result_ready")
        stored = sem("stored")

        in_bank = [turn_in, back_bank]

        def row_bank(t, alone):
            return turn_in if alone and t % 2 else back_bank

        INPUTS_AT = (2, 6)
        SPLITS_AT = 2

        PIECES = 4
        PW = HALVES * HID // PIECES

        def w1_block(t, k, c):
            return t[:, k * HID + c * P:k * HID + (c + 1) * P]

        def w2_block(t, c, m):
            return t[:, c * DM + m * P:c * DM + (m + 1) * P]

        block = stack.enter_context(nc.Block())

        @block.sync
        def _(sp):
            sp.dma_start(kern_sb[:, P:P + L], ssm_kernel).then_inc(kern_loaded, 16)
            sp.dma_start(D_sb[:], D_skip.rearrange("(h a) -> h a", a=1)).then_inc(kern_loaded, 16)
            for q in range(2):
                part = slice(q * GB, (q + 1) * GB)
                sp.dma_start(x_sb[:, part, :], x[part].rearrange("b s d -> s b d")).then_inc(x_loaded[q], 16)
            for q in range(2):
                part = slice(q * GB, (q + 1) * GB)
                sp.dma_start(ctx_sb[:, part, :], ctx[part].rearrange("b s d -> s b d")).then_inc(ctx_loaded[q], 16)
            sp.wait_ge(kern_padded, 1)

            def skew(n):
                heads = slice(SKEW * n, SKEW * (n + 1))
                dst = bass.AP(skewed.tensor, SKEW * n * P * (ROW + 1),
                              [[P * (ROW + 1), SKEW], [ROW + 1, P], [1, ROW]])
                sp.dma_start(dst, kern_sb[heads, :].unsqueeze(1).broadcast_to([SKEW, P, ROW])
                             ).then_inc(kern_in_dram[n], 16)

            def load_toeplitz(j, ring):
                for i in range(HEAD_RING):
                    if isinstance(j, int) and i % SKEW == 0:
                        sp.wait_ge(kern_in_dram[(HEAD_RING * j + i) // SKEW], 16)
                    if ring:
                        sp.wait_ge(kv_used, HEAD_RING * (j - 1) + i + 1)
                    src = skewed[bass.ds(HEAD_RING * j + i, 1), 0:P * ROW].rearrange("a (m l) -> (a m) l", m=P)
                    sp.dma_start(toep[i][:], src[:, P:P + L]).then_inc(toep_loaded[i], 16)

            skew(0)
            skew(1)
            sp.dma_start(gates2[:, 0:1], g_xattn.rearrange("(a b) -> a b", a=1).broadcast_to([P, 1])
                         ).then_inc(consts_loaded, 16)
            sp.dma_start(gates2[:, 1:2], g_ffn.rearrange("(a b) -> a b", a=1).broadcast_to([P, 1])
                         ).then_inc(consts_loaded, 16)
            sp.dma_start(gate_sb[:], gating_w.rearrange("(k p) e -> p k e", p=P)).then_inc(consts_loaded, 16)
            sp.dma_start(bias_rows[0:E * CH, :], b1.rearrange("e (c p) -> (e c) p", p=P)).then_inc(consts_loaded, 16)
            sp.dma_start(bias_rows[E * CH:, :], b2.rearrange("e (c p) -> (e c) p", p=P)).then_inc(consts_loaded, 16)
            load_toeplitz(0, False)
            skew(2)
            skew(3)
            load_toeplitz(1, True)
            for n in range(4, H // SKEW):
                skew(n)

            def load_weights(g, a):
                n = 2 * g + a
                sp.dma_start(w_raw[a][0][:].rearrange("p (k h) -> p k h", k=HALVES),
                             w1[bass.ds(n, 1)].rearrange("e (k p) h -> p (e k) h", p=P)
                             ).then_inc(w_loaded[a][0], 16)
                sp.dma_start(w_raw[a][1][:].rearrange("p (c d) -> p c d", c=CH),
                             w2[bass.ds(n, 1)].rearrange("e (c p) d -> p (e c) d", p=P)
                             ).then_inc(w_loaded[a][1], 16)

            for n in range(4, H // SKEW):
                sp.wait_ge(kern_in_dram[n], 16)
            with sp.Fori(2, HEAD_LOOPS) as j:
                load_toeplitz(j, True)
            load_weights(0, 0)
            sp.wait_ge(zeroed, 1)
            for k in range(TOP_K):
                sp.dma_start(picks_dram[k * T:(k + 1) * T].rearrange("(b s) d -> s b d", s=S),
                             zeros[:].unsqueeze(1).broadcast_to([P, B, DM])
                             ).then_inc(picks_zeroed, 16)
            for q in range(2):
                part = slice(q * GB, (q + 1) * GB)
                sp.wait_ge(xn_ready[q], GB)
                sp.dma_start(tokens_dram.rearrange("(b s) d -> s b d", s=S)[:, part, :], xn_sb[:, part, :]
                             ).then_inc(xn_stored, 16)
            sp.wait_ge(summed, HALVES * H)
            load_weights(0, 1)
            with sp.Fori(1, PAIRS) as g:
                for a in range(2):
                    sp.wait_ge(w1_lo_ready, PIECES * (2 * g + a - 1))
                    sp.wait_ge(w2_lo_ready, PIECES * (2 * g + a - 1))
                    load_weights(g, a)
            sp.wait_ge(scattered, 16 * TILES)
            for q in range(ENDS):
                part = slice(q * EB, (q + 1) * EB)
                for k in range(TOP_K):
                    src = picks_dram[k * T:(k + 1) * T].rearrange("(b s) d -> s b d", s=S)
                    sp.dma_start(picks[k][:, part, :], src[:, part, :]).then_inc(picks_loaded[q], 16)
            for q in range(ENDS):
                part = slice(q * EB, (q + 1) * EB)
                sp.wait_ge(result_ready, EB * (q + 1))
                sp.dma_start(out[part].rearrange("b s d -> s b d"), xn_sb[:, part, :]).then_inc(stored, 16)
            sp.wait_ge(stored, 16 * ENDS)

        @block.gpsimd
        def _(pool):
            nc.gpsimd.memset(ident[:], 0.0).then_inc(pool_step, 1)
            nc.gpsimd.memset(ones[:], 1.0).then_inc(pool_step, 1)
            pool.wait_ge(pool_step, 2)
            nc.gpsimd.affine_select(out=ident[:], in_=ident[:], pattern=[[-1, P]], compare_op=ALU.not_equal,
                                    fill=1.0, base=0, channel_multiplier=1).then_inc(consts_made, 1)
            nc.gpsimd.affine_select(out=before[:], in_=ones[:], pattern=[[1, P]], compare_op=ALU.is_gt,
                                    fill=0.0, base=0, channel_multiplier=-1).then_inc(consts_made, 1)
            nc.gpsimd.iota(expert_iota[:], [[1, E]], base=0, channel_multiplier=0,
                           allow_small_or_imprecise_dtypes=True).then_inc(consts_made, 1)
            nc.gpsimd.iota(tile_iota[:], [[1, TILES]], base=0, channel_multiplier=0,
                           allow_small_or_imprecise_dtypes=True).then_inc(consts_made, 1)
            nc.gpsimd.iota(col_iota[:], [[1, P]], base=0, channel_multiplier=0,
                           allow_small_or_imprecise_dtypes=True).then_inc(consts_made, 1)
            nc.gpsimd.iota(item_id[:], [[S, B], [T, TOP_K]], base=1, channel_multiplier=1,
                           allow_small_or_imprecise_dtypes=True).then_inc(consts_made, 1)
            nc.gpsimd.memset(minus_half[:], -0.5).then_inc(pool_step, 1)
            nc.gpsimd.memset(ones_f, 1.0).then_inc(consts_made, 1)
            nc.gpsimd.memset(zeros[:], 0.0).then_inc(zeroed, 1)

            def make_kv(j, first):
                for i in range(HEAD_RING):
                    h = HEAD_RING * j + i
                    if not first or i >= KV_RING:
                        pool.wait_ge(kv_used, h - KV_RING + 1)
                    for half in range(HALVES):
                        if first and i == 0:
                            pool.wait_ge(turn_out, 2 * (half + 1))
                        c = ctxT[:, half, :, bass.ds(HEAD_DIM * h, HEAD_DIM)]
                        quads = by_pair(kv[i % KV_RING][:, half, :])
                        for quad in QUADS:
                            rows_of, cols_of = quad[2:]
                            shape = [P, B, HB, cols_of.stop - cols_of.start]
                            last = nc.gpsimd.tensor_tensor(
                                quads[quad],
                                c[:, :, rows_of].unsqueeze(3).broadcast_to(shape),
                                c[:, :, cols_of].unsqueeze(2).broadcast_to(shape), ALU.mult)
                        last.then_inc(kv_ready, 1)
                        if half == 0 and HALVES * (i - POOL_LAG) + 1 == POOL_ITEM:
                            k = POOL_ITEM % PROD_RING
                            pool.wait_ge(conv_kept, HALVES * (h - POOL_LAG + 1))
                            nc.gpsimd.tensor_tensor(by_pair(prod[k]), by_pair(prod[k]), queries(h - POOL_LAG, 1),
                                                    ALU.mult).then_inc(pool_multiplied, 1)

            def inverse_deviation(count):
                pool.wait_ge(variance_ready, count)
                group = slice(GB * ((count - 1) % 2), GB * ((count - 1) % 2 + 1))
                nc.gpsimd.tensor_tensor(rstd[:, group], rstd[:, group], minus_half[:, group], ALU.pow
                                        ).then_inc(rstd_ready, 1)

            pool.wait_ge(pool_step, 3)
            inverse_deviation(1)
            inverse_deviation(2)
            make_kv(0, True)
            with pool.Fori(1, HEAD_LOOPS) as j:
                make_kv(j, False)

            def w2_piece(n, a, q):
                pool.wait_ge(w_hi_ready, 2 * PIECES * n + PIECES + q + 1)
                cols = slice(q * PW, (q + 1) * PW)
                nc.gpsimd.tensor_tensor(w_lo[a][1][:, cols], w_raw[a][1][:, cols],
                                        w_hi[a][1][:, cols].bitcast(F32), ALU.subtract).then_inc(w2_lo_ready, 1)

            last_token = nc.gpsimd.to_reg(T - 1)
            last_pick = nc.gpsimd.to_reg(TOP_K * T - 1)

            def gather(g, tiles):
                for t in tiles:
                    nc.gpsimd.indirect_dma_start(
                        gathered[:, t, :], None, tokens_dram,
                        bass.IndirectOffsetOnAxis(ap=source_row[:, TPP * g + t:TPP * g + t + 1], axis=0),
                        bounds_check=last_token, oob_is_err=False).then_inc(gather_a if t < 3 else gather_b, 16)

            def scatter(g, t):
                pool.wait_ge(row_ready, TPP * g + t + 1)
                nc.gpsimd.indirect_dma_start(
                    picks_dram, bass.IndirectOffsetOnAxis(ap=target_row[:, TPP * g + t:TPP * g + t + 1], axis=0),
                    rows[:, t, :], None,
                    bounds_check=last_pick, oob_is_err=False).then_inc(scattered, 16)

            for q in range(2):
                inverse_deviation(3 + q)
                pool.wait_ge(rstd_ready, 3 + q)
                part = slice(q * GB, (q + 1) * GB)
                nc.gpsimd.tensor_tensor(shift[:, part], neg_mean[:, part], rstd[:, part], ALU.mult
                                        ).then_inc(shift_ready, 1)
            for q in range(PIECES):
                w2_piece(0, 0, q)
            pool.wait_ge(slot_col_ready, 1)
            for r in range(NR - POOL_HOTS, NR):
                nc.gpsimd.tensor_scalar(col_hot[:, r, :], col_iota[:], slot_col[:, r // TOP_K, r % TOP_K:r % TOP_K + 1], None,
                                        ALU.is_equal).then_inc(pool_hots, 1)
            pool.wait_ge(xn_stored, 16 * 2)
            pool.wait_ge(rows_known, 2)
            gather(0, range(TPP))
            pool.wait_ge(picks_zeroed, 16 * TOP_K)
            for g in range(PAIRS):
                for q in range(PIECES):
                    if g > 0 and q < TPP - 2:
                        scatter(g - 1, 2 + q)
                    w2_piece(2 * g + 1, 1, q)
                if g < PAIRS - 1:
                    pool.wait_ge(in_turned, HALVES * (2 * g + 2))
                    gather(g + 1, range(TPP))
                for q in range(PIECES):
                    if q < 2:
                        scatter(g, q)
                    if g < PAIRS - 1:
                        w2_piece(2 * g + 2, 0, q)
            for t in range(2, TPP):
                scatter(PAIRS - 1, t)

        @block.tensor
        def _(pe):
            def turn(use, src, half, b0):
                wait_for(pe, turn_out, use - 3)
                for q in range(4):
                    b = b0 + q
                    last = pe.transpose(turn_bank[use % 4][:, q * P:(q + 1) * P],
                                        src[:, b, half * P:(half + 1) * P], ident[:])
                last.then_inc(turned, 1)

            def place_x(q):
                pe.wait_ge(x_loaded[q], 16)
                for b in range(q * GB, (q + 1) * GB):
                    pe.matmul(x2_bank[b // 2][:, (b % 2) * DM:(b % 2 + 1) * DM], ident[:], x_sb[:, b, :],
                              start=(b % 2 == 0), stop=False, skip_group_check=True)

            pe.wait_ge(consts_made, 1)
            place_x(0)
            use = 0
            for half in range(HALVES):
                for b0 in (0, GB):
                    pe.wait_ge(ctx_loaded[b0 // GB], 16)
                    turn(use, ctx_sb, half, b0)
                    use += 1
            for b0 in (0, GB):
                pe.wait_ge(q_ready, b0 + GB)
                for half in range(HALVES):
                    turn(use, xn_sb, half, b0)
                    use += 1
            pe.wait_ge(consts_loaded, 16 * 5)
            NB = E * (CH + HALVES)
            pe.wait_ge(turn_out, 5)
            pe.transpose(turn_bank[0][:, 0:NB], bias_rows[:], ident[0:NB, 0:NB]).then_inc(turned, 1)
            pe.wait_ge(turn_out, 6)
            pe.wait_ge(consts_made, 7)
            for half in range(HALVES):
                last = pe.matmul(turn_bank[1][:, B * E:(B + 1) * E], ones_f, gate_sb[:, half, :],
                                 start=(half == 0), stop=(half == HALVES - 1), skip_group_check=True)
            last.then_inc(gate_summed, 1)

            def convolve(j, first):
                for i in range(HEAD_RING):
                    h = HEAD_RING * j + i
                    pe.wait_ge(toep_loaded[i], 16 * (j + 1))
                    if first and i == 1:
                        pe.wait_ge(turn_out, 8)
                    y0, y1 = conv_bank[2 * (i % 2)], conv_bank[2 * (i % 2) + 1]
                    if not first or i >= 2:
                        pe.wait_ge(conv_kept, HALVES * (h - 1))
                    for y, taps, half in ((y0, slice(0, P), 0), (y1, slice(P, L), 0), (y1, slice(0, P), 1)):
                        if taps.start == 0:
                            pe.wait_ge(kv_ready, HALVES * h + half + 1)
                        for q, quad in enumerate(QUADS):
                            last = pe.matmul(by_pair(y[:])[quad], toep[i][:, taps],
                                             by_pair(kv[i % KV_RING][:, half, :])[quad],
                                             start=(half == 0 and q == 0), stop=True, skip_group_check=True)
                        if y is y0:
                            last.then_inc(conv_ready, 1)
                    last.then_inc(kv_used, 1)

            def gate_queries(batches):
                for b in batches:
                    for half in range(HALVES):
                        last = pe.matmul(turn_bank[1][:, b * E:(b + 1) * E], qT[:, half, b, :], gate_sb[:, half, :],
                                         start=False, stop=(half == 1), skip_group_check=True)
                last.then_inc(queries_gated, 1)

            convolve(0, True)
            pe.wait_ge(gate_centered, 1)
            gate_queries(range(GB))
            with pe.Fori(1, HEAD_LOOPS - 1) as j:
                convolve(j, False)
            gate_queries(range(GB, B))
            convolve(HEAD_LOOPS - 1, False)

            pe.wait_ge(act_step, 1)
            pe.wait_ge(old_logits_ready, 1)
            place_x(1)
            pe.wait_ge(gate_scaled, 2)
            for i in range(B // 2):
                for half in range(HALVES):
                    pe.wait_ge(summed, HALVES * (H - 1) + half + 1)
                    for b in (2 * i, 2 * i + 1):
                        col = (b % 2) * DM + half * P
                        last = pe.matmul(x2_bank[i][:, col:col + P], attnT[:, half, b, :], scaled_ident,
                                         start=False, stop=(b % 2 == 1 and half == 1), skip_group_check=True)
                last.then_inc(x2_ready, 1)
            for b in range(B):
                for half in range(HALVES):
                    last = pe.matmul(gate_bank[:, b * E:(b + 1) * E], attnT[:, half, b, :], scaled_gate[:, half, :],
                                     start=(b == half == 0), stop=(half == 1), skip_group_check=True)
            last.then_inc(gated, 1)

            pe.wait_ge(taken_ready, 1)
            flat = taken[:].rearrange("p b e -> p (b e)")
            for b in range(B - 1):
                pe.matmul(pos_bank[:, (b + 1) * E:B * E], ones[:],
                          taken[:, b:b + 1, :].broadcast_to([P, B - 1 - b, E]),
                          start=(b == 0), stop=False, skip_group_check=True)
            pe.matmul(pos_bank[:, 0:B * E], before[:], flat, start=False, stop=True, skip_group_check=True
                      ).then_inc(positions_ready, 1)
            pe.wait_ge(tiles_marked, 1)
            for r in range(NR):
                if r < NR - POOL_HOTS:
                    pe.wait_ge(dve_hots, r + 1)
                else:
                    pe.wait_ge(pool_hots, r - (NR - POOL_HOTS) + 1)
                last = pe.matmul(gate_bank[:, 128:128 + TILES], col_hot[:, r, :], tile_ids[:, r, :],
                                 start=(r == 0), stop=(r == NR - 1))
            last.then_inc(table_ready, 1)

            def inputs(g, a, half):
                if half == 0:
                    pe.wait_ge(gather_a, 16 * 3 * (g + 1))
                    if a == 1:
                        pe.wait_ge(gather_b, 16 * 2 * (g + 1))
                wait_for(pe, in_lo_ready, HALVES * (2 * g + a))
                if half == 1:
                    wait_for(pe, row_ready, TPP * g - 3)
                if a == 0:
                    pieces = [(0, 0, P, 0), (1, 0, P, P), (2, 0, P // 2, 2 * P)]
                else:
                    pieces = [(3, 0, P, P // 2), (4, 0, P, P // 2 + P), (2, P // 2, P, 0)]
                for t, p0, p1, col in pieces:
                    last = pe.transpose(in_bank[half][:, col:col + p1 - p0],
                                        gathered[p0:p1, t, half * P:(half + 1) * P], ident[p0:p1, p0:p1])
                last.then_inc(in_turned, 1)

            def up(n, a, c):
                if c == 0:
                    pe.wait_ge(in_lo_ready, HALVES * (n + 1))
                    pe.wait_ge(w_hi_ready, 2 * PIECES * n + PIECES)
                    pe.wait_ge(w1_lo_ready, PIECES * (n + 1))
                wait_for(pe, hid_ready, CH * n + c - 1)
                bankc = up_bank[c % 2][:, 0:CAP]
                for k in range(HALVES):
                    hi, lo = w1_block(w_hi[a][0], k, c), w1_block(w_lo[a][0], k, c)
                    pe.matmul(bankc, hi, in_hi[a][:, k, :], start=(k == 0), stop=False)
                    pe.matmul(bankc, hi, in_lo[a][:, k, :], start=False, stop=False)
                    last = pe.matmul(bankc, lo, in_hi[a][:, k, :], start=False, stop=(k == HALVES - 1))
                last.then_inc(up_done, 1)

            def down(n, a, c):
                if c == 0:
                    pe.wait_ge(w_hi_ready, 2 * PIECES * (n + 1))
                    pe.wait_ge(w2_lo_ready, PIECES * (n + 1))
                    wait_for(pe, outT_ready, n - 1)
                pe.wait_ge(hid_lo_ready, CH * n + c + 1)
                for m in range(HALVES):
                    hi, lo = w2_block(w_hi[a][1], c, m), w2_block(w_lo[a][1], c, m)
                    bankm = down_bank[a][m][:, 0:CAP]
                    pe.matmul(bankm, hi, hid_hi[c % HR][:], start=(c == 0), stop=False)
                    pe.matmul(bankm, hi, hid_lo[c % HR][:], start=False, stop=False)
                    last = pe.matmul(bankm, lo, hid_hi[c % HR][:], start=False, stop=(c == CH - 1))
                last.then_inc(down_done, 1)

            def back(g, t, alone=False):
                if t == 0:
                    pe.wait_ge(outT_ready, 2 * g + 1)
                if t == 2:
                    pe.wait_ge(outT_ready, 2 * g + 2)
                if t == 2 and not alone:
                    pe.wait_ge(in_lo_ready, HALVES * (2 * g + 4))
                wait_for(pe, row_ready, TPP * g + t - (1 if alone else 0))
                for half in range(HALVES):
                    last = pe.transpose(row_bank(t, alone)[:, half * P:(half + 1) * P],
                                        outT[:, half, t * P:(t + 1) * P], ident[:])
                last.then_inc(out_turned, 1)

            def pair(g, first, last):
                for a in range(2):
                    n = 2 * g + a
                    for c in range(CH):
                        up(n, a, c)
                        if c >= 2:
                            down(n, a, c - 2)
                        elif a == 1 or not first:
                            down(n - 1, 1 - a, c + CH - 2)
                        if a == 0 and not first and 3 <= c < 6:
                            back(g - 1, c - 1)
                        if a == 1 and 3 <= c < 5:
                            back(g, c - 3)
                        if c == INPUTS_AT[a] and not (last and a == 1):
                            for half in range(HALVES):
                                inputs(g + a, 1 - a, half)

            pe.wait_ge(rows_known, 2)
            pe.wait_ge(x2_kept, B // 2)
            inputs(0, 0, 0)
            inputs(0, 0, 1)
            pair(0, True, False)
            with pe.Fori(1, PAIRS - 1) as g:
                pair(g, False, False)
            pair(PAIRS - 1, False, True)
            down(E - 1, 1, CH - 2)
            down(E - 1, 1, CH - 1)
            for t in range(2, TPP):
                back(PAIRS - 1, t, alone=True)

        @block.scalar
        def _(act):
            for use in range(8):
                dst, half, b0 = (ctxT, use // 2, GB * (use % 2)) if use < 4 else (qT, use % 2, GB * (use // 2 - 2))
                act.wait_ge(turned, use + 1)
                nc.scalar.copy(dst[:, half, b0:b0 + GB, :].rearrange("p b c -> p (b c)"),
                               turn_bank[use % 4][:]).then_inc(turn_out, 1)
            act.wait_ge(consts_loaded, 16 * 5)
            nc.scalar.activation(tanh2[:], gates2[:], ACT.Tanh).then_inc(tanh_ready, 1)
            act.wait_ge(turned, 9)
            nc.scalar.copy(biasT[:], turn_bank[0][:, 0:E * (CH + HALVES)]).then_inc(act_step, 1)
            act.wait_ge(tanh_ready, 1)
            nc.scalar.activation(scaled_ident, ident[:], ACT.Identity, scale=tanh2[:, 0:1]).then_inc(gate_scaled, 1)
            act.wait_ge(gate_centered, 1)
            nc.scalar.activation(scaled_gate[:], gate_c[:], ACT.Identity, scale=tanh2[:, 0:1]
                                 ).then_inc(gate_scaled, 1)

            def keep(j, first):
                for k in range(HALVES * HEAD_RING):
                    h = HEAD_RING * j + k // HALVES
                    act.wait_ge(kv_used if k % HALVES else conv_ready, h + 1)
                    if not first or k >= PROD_RING:
                        act.wait_ge(summed, HALVES * HEAD_RING * j + k - PROD_RING + 1)
                    y, kept = by_pair(conv_bank[k % 4][:]), by_pair(prod[k % PROD_RING])
                    nc.scalar.copy(kept[:, :, 0:HB, :], y[:, :, 0:HB, :])
                    nc.scalar.copy(kept[:, :, HB:, :], y[:, :, :, HB:].rearrange("p b i j -> p b j i")
                                   ).then_inc(conv_kept, 1)

            keep(0, True)
            with act.Fori(1, HEAD_LOOPS) as j:
                keep(j, False)

            def split(g, a, piece):
                m, q = piece // PIECES, piece % PIECES
                n = 2 * g + a
                if q == 0:
                    act.wait_ge(w_loaded[a][m], 16 * (g + 1))
                    if m == 0:
                        wait_for(act, up_done, CH * (n - 1))
                    else:
                        wait_for(act, down_done, CH * (n - 1))
                cols = slice(q * PW, (q + 1) * PW)
                nc.scalar.copy(w_hi[a][m][:, cols], w_raw[a][m][:, cols]).then_inc(w_hi_ready, 1)

            def input_high(g, a, half):
                n2 = 2 * (2 * g + a) + half
                act.wait_ge(in_turned, n2 + 1)
                if half == 0:
                    wait_for(act, up_done, CH * (2 * g + a - 1))
                nc.scalar.copy(in_hi[a][:, half, :], in_bank[half][:, 0:CAP]).then_inc(in_hi_ready, 1)

            def hidden(n, c):
                act.wait_ge(up_done, CH * n + c + 1)
                wait_for(act, hid_lo_ready, CH * n + c - 1)
                nc.scalar.activation(hid[c % 2][:], up_bank[c % 2][:, 0:CAP], ACT.Relu,
                                     bias=biasT[:, bass.ds(CH * n + c, 1)]).then_inc(hid_ready, 1)

            def output(n, a, g):
                act.wait_ge(down_done, CH * (n + 1))
                wait_for(act, out_turned, TPP * g)
                for m in range(HALVES):
                    last = nc.scalar.activation(outT[:, m, a * CAP:(a + 1) * CAP], down_bank[a][m][:, 0:CAP],
                                                ACT.Identity, bias=biasT[:, bass.ds(E * CH + HALVES * n + m, 1)])
                last.then_inc(outT_ready, 1)

            for piece in range(2 * PIECES):
                split(0, 0, piece)
            def normalize(q):
                act.wait_ge(shift_ready, q + 1)
                for b in range(q * GB, (q + 1) * GB):
                    nc.scalar.activation(xn_sb[:, b, :], x2_bank[b // 2][:, (b % 2) * DM:(b % 2 + 1) * DM],
                                         ACT.Identity, bias=shift[:, b:b + 1], scale=rstd[:, b:b + 1]
                                         ).then_inc(xn_ready[q], 1)

            normalize(0)
            act.wait_ge(shifted, 1)
            nc.scalar.activation(probs[:], logits[:], ACT.Exp).then_inc(exp_ready, 1)
            normalize(1)
            for i in range(B // 2):
                nc.scalar.copy(x_sb[:, 2 * i:2 * i + 2, :].rearrange("p b d -> p (b d)"), x2_bank[i][:]
                               ).then_inc(x2_kept, 1)
            act.wait_ge(act_step, 1)
            input_high(0, 0, 0)
            input_high(0, 0, 1)

            def pair(g, first, last):
                for a in range(2):
                    n = 2 * g + a
                    for c in range(CH):
                        hidden(n, c)
                        if c == 1 and (a == 1 or not first):
                            output(n - 1, 1 - a, g if a == 1 else g - 1)
                        if c >= 1 and not (last and a == 1):
                            g2, a2 = (g, 1) if a == 0 else (g + 1, 0)
                            if c == INPUTS_AT[a]:
                                for half in range(HALVES):
                                    input_high(g2, a2, half)
                            if 0 <= c - SPLITS_AT < PIECES:
                                split(g2, a2, 2 * (c - SPLITS_AT))
                                split(g2, a2, 2 * (c - SPLITS_AT) + 1)

            pair(0, True, False)
            with act.Fori(1, PAIRS - 1) as g:
                pair(g, False, False)
            pair(PAIRS - 1, False, True)
            output(E - 1, 1, PAIRS - 1)

        @block.vector
        def _(dve):
            steps = [0]

            def step(ins):
                steps[0] += 1
                ins.then_inc(dve_step, 1)
                dve.wait_ge(dve_step, steps[0])

            step(nc.vector.memset(kern_sb[:, 0:P], 0.0))
            dve.wait_ge(kern_loaded, 32)
            nc.vector.tensor_tensor(kern_sb[:, P:P + 1], kern_sb[:, P:P + 1], D_sb[:], ALU.add
                                    ).then_inc(kern_padded, 1)

            def of_batch(source, b):
                if source is x_sb:
                    return x_sb[:, b, :]
                return source[b // 2][:, (b % 2) * DM:(b % 2 + 1) * DM]

            def statistics(group, source):
                for b in group:
                    if source is not x_sb:
                        dve.wait_ge(x2_ready, b // 2 + 1)
                    last = nc.vector.bn_stats(stats[:, b, :], of_batch(source, b))
                step(last)
                for b in group:
                    last = nc.vector.bn_aggr(moments[:, b, :], stats[:, b, :])
                step(last)
                cols = slice(group[0], group[-1] + 1)
                nc.vector.tensor_scalar(neg_mean[:, cols], moments[:, cols, 0], -1.0, None, ALU.mult)
                nc.vector.tensor_scalar(rstd[:, cols], moments[:, cols, 1], LN_EPS, None, ALU.add
                                        ).then_inc(variance_ready, 1)

            def normalize(group, count, ready):
                dve.wait_ge(rstd_ready, count)
                for b in group:
                    nc.vector.tensor_scalar(xn_sb[:, b, :], x_sb[:, b, :], moments[:, b, 0:1], rstd[:, b:b + 1],
                                            ALU.subtract, ALU.mult).then_inc(ready, 1)

            groups = [range(q * GB, (q + 1) * GB) for q in range(2)]
            for q in range(2):
                dve.wait_ge(x_loaded[q], 16)
                statistics(groups[q], x_sb)
            for q in range(2):
                normalize(groups[q], q + 1, q_ready)
            nc.vector.reciprocal(deviation[:], rstd[:])
            dve.wait_ge(gate_summed, 1)
            nc.vector.scalar_tensor_tensor(
                out=gate_c[:], in0=turn_bank[1][:, B * E:(B + 1) * E].unsqueeze(1).broadcast_to([P, HALVES, E]),
                scalar=-1.0 / DM, in1=gate_sb[:], op0=ALU.mult, op1=ALU.add).then_inc(gate_centered, 1)

            ITEMS = HALVES * HEAD_RING
            def multiply(j, k):
                h, half = HEAD_RING * j + k // HALVES, k % HALVES
                dve.wait_ge(conv_kept, ITEMS * j + k + 1)
                p = by_pair(prod[k % PROD_RING])
                nc.vector.tensor_tensor(p, p, queries(h, half), ALU.mult).then_inc(multiplied, 1)

            def add_up(j, k):
                h, half = HEAD_RING * j + k // HALVES, k % HALVES
                if k == POOL_ITEM:
                    dve.wait_ge(pool_multiplied, j + 1)
                else:
                    dve.wait_ge(multiplied, (ITEMS - 1) * j + k + (1 if k < POOL_ITEM else 0))
                nc.vector.tensor_reduce(attnT[:, half, :, bass.ds(HEAD_DIM * h, HEAD_DIM)],
                                        by_pair(prod[k % PROD_RING]),
                                        AX_X, ALU.add).then_inc(summed, 1)

            def attend(j, first):
                for k in range(ITEMS):
                    if k != POOL_ITEM:
                        multiply(j, k)
                    if k >= SUM_LAG:
                        add_up(j, k - SUM_LAG)
                    elif not first:
                        add_up(j - 1, ITEMS + k - SUM_LAG)

            dve.wait_ge(turn_out, 8)
            attend(0, True)
            with dve.Fori(1, HEAD_LOOPS - 1) as j:
                attend(j, False)
            dve.wait_ge(queries_gated, 2)
            of_tokens = [P, B, E]
            nc.vector.tensor_tensor(logits[:], turn_bank[1][:, 0:B * E].rearrange("p (b e) -> p b e", b=B),
                                    deviation[:].unsqueeze(2).broadcast_to(of_tokens), ALU.mult
                                    ).then_inc(old_logits_ready, 1)
            attend(HEAD_LOOPS - 1, False)
            for k in range(ITEMS - SUM_LAG, ITEMS):
                add_up(HEAD_LOOPS - 1, k)

            for q in range(2):
                statistics(groups[q], x2_bank)

            def w1_split(g, a, q):
                n = 2 * g + a
                dve.wait_ge(w_hi_ready, 2 * PIECES * n + q + 1)
                cols = slice(q * PW, (q + 1) * PW)
                nc.vector.tensor_tensor(w_lo[a][0][:, cols], w_raw[a][0][:, cols],
                                        w_hi[a][0][:, cols].bitcast(F32), ALU.subtract).then_inc(w1_lo_ready, 1)

            dve.wait_ge(gated, 1)
            dve.wait_ge(old_logits_ready, 1)
            bc = of_tokens
            step(nc.vector.tensor_tensor(logits[:], gate_bank[:, 0:B * E].rearrange("p (b e) -> p b e", b=B),
                                         logits[:], ALU.add))
            dve.wait_ge(rstd_ready, 4)
            step(nc.vector.tensor_tensor(logits[:], logits[:], rstd[:].unsqueeze(2).broadcast_to(bc), ALU.mult))
            step(nc.vector.tensor_reduce(small[:, 0, :], logits[:], AX_X, ALU.max))
            nc.vector.tensor_tensor(logits[:], logits[:], small[:, 0, :].unsqueeze(2).broadcast_to(bc), ALU.subtract
                                    ).then_inc(shifted, 1)
            dve.wait_ge(exp_ready, 1)
            step(nc.vector.tensor_reduce(small[:, 1, :], probs[:], AX_X, ALU.add))
            step(nc.vector.reciprocal(small[:, 2, :], small[:, 1, :]))
            step(nc.vector.tensor_tensor(probs[:], probs[:], small[:, 2, :].unsqueeze(2).broadcast_to(bc), ALU.mult))
            for b in range(B):
                last = nc.vector.max(top8[:, b, :], probs[:, b, :])
            step(last)
            for b in range(B):
                last = nc.vector.max_index(top8_at[:, b, :], top8[:, b, :], probs[:, b, :])
            step(last)
            nc.vector.tensor_copy(chosen[:], top8_at[:, :, 0:TOP_K])
            dve.wait_ge(consts_made, 6)
            bke = [P, B, TOP_K, E]
            step(nc.vector.tensor_tensor(onehot[:], top8_at[:, :, 0:TOP_K].unsqueeze(3).broadcast_to(bke),
                                         expert_iota[:].unsqueeze(1).unsqueeze(1).broadcast_to(bke), ALU.is_equal))
            nc.vector.tensor_tensor(taken[:], onehot[:, :, 0], onehot[:, :, 1], ALU.add).then_inc(taken_ready, 1)
            dve.wait_ge(positions_ready, 1)
            pos = pos_bank[:, 0:B * E].rearrange("p (b e) -> p b e", b=B)
            step(nc.vector.tensor_tensor(before_me[:], onehot[:], pos.unsqueeze(2).broadcast_to(bke), ALU.mult))
            step(nc.vector.tensor_reduce(position[:], before_me[:], AX_X, ALU.add))
            nc.vector.tensor_scalar(dropped[:], position[:], float(CAP), OUT_OF_BOUNDS, ALU.is_ge, ALU.mult)
            step(nc.vector.scalar_tensor_tensor(out=slot[:], in0=chosen[:], scalar=float(CAP), in1=position[:],
                                                op0=ALU.mult, op1=ALU.add))
            step(nc.vector.tensor_tensor(slot_i[:], slot[:], dropped[:], ALU.add))
            nc.vector.tensor_scalar(slot_tile_i[:], slot_i[:], 7, None, ALU.logical_shift_right)
            step(nc.vector.tensor_scalar(slot_col_i[:], slot_i[:], P - 1, None, ALU.bitwise_and))
            nc.vector.tensor_copy(slot_col[:], slot_col_i[:]).then_inc(slot_col_ready, 1)
            bt = [P, NR, TILES]
            step(nc.vector.tensor_tensor(tile_hot[:], slot_tile_i[:].rearrange("p b k -> p (b k)").unsqueeze(2).broadcast_to(bt),
                                         tile_iota[:].unsqueeze(1).broadcast_to(bt), ALU.is_equal))
            nc.vector.tensor_tensor(tile_ids[:], tile_hot[:],
                                    item_id[:].rearrange("p b k -> p (b k)").unsqueeze(2).broadcast_to(bt),
                                    ALU.mult).then_inc(tiles_marked, 1)
            dve.wait_ge(slot_col_ready, 1)
            for r in range(NR - POOL_HOTS):
                nc.vector.tensor_scalar(col_hot[:, r, :], col_iota[:], slot_col[:, r // TOP_K, r % TOP_K:r % TOP_K + 1], None,
                                        ALU.is_equal).then_inc(dve_hots, 1)
            dve.wait_ge(table_ready, 1)
            table = gate_bank[:, 128:128 + TILES]
            nc.vector.tensor_scalar(table_a[:], table, float(T), -float(T), ALU.is_gt, ALU.mult)
            nc.vector.tensor_scalar(table_b[:], table, 1.0, -1.0, ALU.max, ALU.add)
            step(nc.vector.tensor_scalar(table_c[:], table, 0.0, OUT_OF_BOUNDS, ALU.is_equal, ALU.mult))
            nc.vector.tensor_tensor(source_row[:], table_b[:], table_a[:], ALU.add).then_inc(rows_known, 1)
            nc.vector.tensor_tensor(target_row[:], table_c[:], table_b[:], ALU.add).then_inc(rows_known, 1)
            both = top8[:, :, 0:TOP_K]
            step(nc.vector.tensor_reduce(small[:, 3, :], both, AX_X, ALU.add))
            step(nc.vector.tensor_scalar(small[:, 3, :], small[:, 3, :], NORM_EPS, None, ALU.add))
            step(nc.vector.reciprocal(small[:, 3, :], small[:, 3, :]))
            nc.vector.tensor_scalar(dropped[:], position[:], float(CAP), tanh2[:, 1:2], ALU.is_lt, ALU.mult)
            step(nc.vector.tensor_tensor(weight[:], both, small[:, 3, :].unsqueeze(2).broadcast_to([P, B, TOP_K]),
                                         ALU.mult))
            step(nc.vector.tensor_tensor(weight[:], weight[:], dropped[:], ALU.mult))
            for q in range(PIECES):
                w1_split(0, 0, q)

            def input_low(g, a, half):
                n2 = 2 * (2 * g + a) + half
                dve.wait_ge(in_hi_ready, n2 + 1)
                nc.vector.tensor_tensor(in_lo[a][:, half, :], in_bank[half][:, 0:CAP],
                                        in_hi[a][:, half, :].bitcast(F32), ALU.subtract).then_inc(in_lo_ready, 1)

            def hidden_split(n, c):
                dve.wait_ge(hid_ready, CH * n + c + 1)
                wait_for(dve, down_done, CH * n + c - HR + 1)
                nc.vector.tensor_copy(hid_hi[c % HR][:], hid[c % 2][:]).then_inc(hid_hi_ready, 1)
                dve.wait_ge(hid_hi_ready, CH * n + c + 1)
                nc.vector.tensor_tensor(hid_lo[c % HR][:], hid[c % 2][:], hid_hi[c % HR][:].bitcast(F32),
                                        ALU.subtract).then_inc(hid_lo_ready, 1)

            def row_tile(g, t, alone=False):
                dve.wait_ge(out_turned, TPP * g + t + 1)
                if t == 0:
                    wait_for(dve, scattered, 16 * TPP * g)
                nc.vector.tensor_copy(rows[:, t, :], row_bank(t, alone)[:, 0:DM]).then_inc(row_ready, 1)

            input_low(0, 0, 0)
            input_low(0, 0, 1)

            def pair(g, first, last):
                for a in range(2):
                    n = 2 * g + a
                    for c in range(CH):
                        hidden_split(n, c)
                        if a == 0 and not first and 3 <= c < 6:
                            row_tile(g - 1, c - 1)
                        if a == 1 and 3 <= c < 5:
                            row_tile(g, c - 3)
                        if c >= 1 and not (last and a == 1):
                            g2, a2 = (g, 1) if a == 0 else (g + 1, 0)
                            if c == INPUTS_AT[a]:
                                for half in range(HALVES):
                                    input_low(g2, a2, half)
                            if 0 <= c - SPLITS_AT < PIECES:
                                w1_split(g2, a2, c - SPLITS_AT)

            pair(0, True, False)
            with dve.Fori(1, PAIRS - 1) as g:
                pair(g, False, False)
            pair(PAIRS - 1, False, True)
            for t in range(2, TPP):
                row_tile(PAIRS - 1, t, alone=True)

            def first_pick(b):
                nc.vector.scalar_tensor_tensor(out=x_sb[:, b, :], in0=picks[0][:, b, :],
                                               scalar=weight[:, b, 0:1], in1=x_sb[:, b, :],
                                               op0=ALU.mult, op1=ALU.add).then_inc(first_added, 1)

            def second_pick(b):
                dve.wait_ge(first_added, b + 1)
                nc.vector.scalar_tensor_tensor(out=xn_sb[:, b, :], in0=picks[1][:, b, :],
                                               scalar=weight[:, b, 1:2], in1=x_sb[:, b, :],
                                               op0=ALU.mult, op1=ALU.add).then_inc(result_ready, 1)

            dve.wait_ge(x2_kept, B // 2)
            for q in range(ENDS):
                dve.wait_ge(picks_loaded[q], 16 * TOP_K)
                for b in range(q * EB, (q + 1) * EB):
                    first_pick(b)
                for b in range(q * EB, (q + 1) * EB):
                    second_pick(b)


_INS = ['x', 'ctx_2048', 'g_xattn', 'g_ffn', 'L0_xattn_ssm_kernel', 'L0_xattn_D', 'L0_ffn_gating_w',
        'L0_ffn_w1', 'L0_ffn_b1', 'L0_ffn_w2', 'L0_ffn_b2']


def kernel(**inputs):
    import numpy as np
    import concourse.bacc as bacc
    from concourse.bass_utils import run_bass_kernel_spmd

    nc = bacc.Bacc("TRN2", target_bir_lowering=False, num_devices=1)
    arrays, args = {}, []
    for name in _INS:
        a = np.ascontiguousarray(inputs[name])
        arrays[f"in_{name}"] = a
        args.append(nc.dram_tensor(f"in_{name}", a.shape, mybir.dt.from_np(a.dtype), kind="ExternalInput").ap())
    out = nc.dram_tensor("out", arrays["in_x"].shape, F32, kind="ExternalOutput").ap()
    build_gated_block(nc, *args, out)
    result = run_bass_kernel_spmd(nc, [arrays], core_ids=[0])
    return result.results[0]["out"]
```

```python
from contextlib import ExitStack

import concourse.bass as bass
from concourse import mybir

F32 = mybir.dt.float32
F32R = mybir.dt.float32r
F16 = mybir.dt.float16
BF16 = mybir.dt.bfloat16
I32 = mybir.dt.int32
U32 = mybir.dt.uint32
ALU = mybir.AluOpType
ACT = mybir.ActivationFunctionType
AX_X = mybir.AxisListType.X

P = 128
HEAD_DIM = 8
TOP_K = 2
LN_EPS = 1e-5
NORM_EPS = 1e-8
OUT_OF_BOUNDS = 8192.0


def wait_for(engine, semaphore, value):
    if not isinstance(value, int) or value > 0:
        engine.wait_ge(semaphore, value)


def build_gated_block(nc, x, ctx, g_xattn, g_ffn, ssm_kernel, D_skip, gating_w, w1, b1, w2, b2, out):
    B, S, DM = x.shape
    H, L = ssm_kernel.shape
    E, _, HID = w1.shape
    HALVES = DM // P
    T = B * S
    CAP = -(-T * TOP_K * 5 // (E * 4))
    SLOTS = E * CAP
    TILES = SLOTS // P
    PAIRS = E // 2
    TPP = TILES // PAIRS
    CH = HID // P
    KVW = B * HEAD_DIM * HEAD_DIM
    HEAD_RING = 4
    KV_RING = 4
    SKEW = 2
    PROD_RING = 8
    SUM_LAG = 2
    HB = HEAD_DIM // 2
    HEAD_LOOPS = H // HEAD_RING
    GB = B // 2
    ENDS = 4
    EB = B // ENDS
    assert S == P and H * HEAD_DIM == P and L == DM and HALVES == 2 and KVW == 512
    assert 2 * CAP == TPP * P and TPP == 5 and CH == 8

    ROW = P + L
    skewed = nc.dram_tensor("skewed_kernels", (H, P * (ROW + 1)), F32, kind="Internal").ap()
    tokens_dram = nc.dram_tensor("tokens_dram", (T, DM), F32, kind="Internal").ap()
    PLANES = TOP_K + 1
    EARLY = TPP * (PAIRS - 1) + 3
    picks_dram = nc.dram_tensor("picks_dram", (PLANES * T, DM), F32, kind="Internal").ap()

    with ExitStack() as stack:
        def sb(name, shape, dt=F32):
            return stack.enter_context(nc.sbuf_tensor(name, shape, dt))

        def ps(name, shape, dt=F32):
            return stack.enter_context(nc.psum_tensor(name, shape, dt))

        def sem(name):
            return stack.enter_context(nc.semaphore(name))

        x_sb = sb("x_sb", [P, B, DM])
        ctx_sb = sb("ctx_sb", [P, B, DM])
        xn_sb = sb("xn_sb", [P, B, DM])
        ctxT = sb("ctxT", [P, HALVES, B, P])
        qT = sb("qT", [P, HALVES, B, P])
        attnT = sb("attnT", [P, HALVES, B, P])
        kern_sb = sb("kern_sb", [H, P + L])
        D_sb = sb("D_sb", [H, 1])
        toep = [sb(f"toep{i}", [P, L]) for i in range(HEAD_RING)]
        kv_space = sb("kv_space", [P, 2 * HALVES * KVW])
        prod_space = sb("prod_space", [P, PROD_RING // 2 * KVW])
        ident = sb("ident", [P, P])
        gate_sb = sb("gate_sb", [P, HALVES, E])
        bias_rows = sb("bias_rows", [E * (CH + HALVES), P])
        biasT = sb("biasT", [P, E * (CH + HALVES)])
        gates2 = sb("gates2", [P, 2])
        tanh2 = sb("tanh2", [P, 2])
        stats = sb("stats", [P, B, 6])
        moments = sb("moments", [P, B, 2])
        rstd = sb("rstd", [P, B])
        minus_half = sb("minus_half", [P, B])
        neg_mean = sb("neg_mean", [P, B])
        shift = sb("shift", [P, B])
        deviation = sb("deviation", [P, B])
        gate_parts = sb("gate_parts", [P, B + 1, E])
        gate_c = sb("gate_c", [P, HALVES, E])
        scaled_gate = sb("scaled_gate", [P, HALVES, E])
        NR = TOP_K * B
        POOL_HOTS = 2
        expert_iota = sb("expert_iota", [P, E])
        tile_iota = sb("tile_iota", [P, TILES])
        col_iota = sb("col_iota", [P, P], F16)
        item_id = sb("item_id", [P, B, TOP_K])
        before = sb("before", [P, P], BF16)
        ones = sb("ones", [P, P], BF16)
        logits = sb("logits", [P, B, E])
        small = sb("small", [P, 4, B])
        probs = sb("probs", [P, B, E])
        top8 = sb("top8", [P, B, 8])
        top8_at = sb("top8_at", [P, B, 8], U32)
        chosen = sb("chosen", [P, B, TOP_K])
        onehot = sb("onehot", [P, B, TOP_K, E])
        taken = sb("taken", [P, B, E], BF16)
        before_me = sb("before_me", [P, B, TOP_K, E])
        position = sb("position", [P, B, TOP_K])
        dropped = sb("dropped", [P, B, TOP_K])
        slot = sb("slot", [P, B, TOP_K])
        slot_i = sb("slot_i", [P, B, TOP_K], I32)
        slot_tile_i = sb("slot_tile_i", [P, B, TOP_K], I32)
        slot_col_i = sb("slot_col_i", [P, B, TOP_K], I32)
        slot_col = sb("slot_col", [P, B, TOP_K])
        weight = sb("weight", [P, B, TOP_K])
        last_parts = sb("last_parts", [P, B, TOP_K])
        last_weight = sb("last_weight", [P, B])
        tile_hot = sb("tile_hot", [P, NR, TILES])
        tile_ids = sb("tile_ids", [P, NR, TILES], F16)
        col_hot = sb("col_hot", [P, NR, P], F16)
        table_a = sb("table_a", [P, TILES])
        table_b = sb("table_b", [P, TILES])
        table_c = sb("table_c", [P, TILES])
        source_row = sb("source_row", [P, TILES], U32)
        half_targets = sb("half_targets", [P, 1], U32)
        target_row = sb("target_row", [P, TILES], U32)
        w_raw = [[sb(f"w{m}_raw{a}", [P, HALVES * HID]) for m in (1, 2)] for a in range(2)]
        w_hi = [[sb(f"w{m}_hi{a}", [P, HALVES * HID], F32R) for m in (1, 2)] for a in range(2)]
        w_lo = [[sb(f"w{m}_lo{a}", [P, HALVES * HID], F32R) for m in (1, 2)] for a in range(2)]
        def in_columns(t, width, n):
            return [t[:, i * width:(i + 1) * width] for i in range(n)]

        kv = [t.rearrange("p (k c) -> p k c", k=HALVES)
              for t in in_columns(kv_space[:], HALVES * KVW, 2) + in_columns(w_raw[1][0][:], HALVES * KVW, 2)]
        prod = (in_columns(prod_space[:], KVW, PROD_RING // 2)
                + in_columns(w_raw[1][1][:], KVW, PROD_RING // 2))
        gathered = ctxT[:].rearrange("p k b c -> p (k b c)")[:, 0:TPP * DM].rearrange("p (t d) -> p t d", t=TPP)
        in_hi = [sb(f"in_hi{a}", [P, HALVES, CAP], F32R) for a in range(2)]
        in_lo = [sb(f"in_lo{a}", [P, HALVES, CAP], F32R) for a in range(2)]
        hid = [sb(f"hid{i}", [P, CAP]) for i in range(2)]
        ones_f = hid[0][:, 0:P]
        scaled_ident = hid[1][:, 0:P]
        HR = 4
        hid_hi = [sb(f"hid_hi{i}", [P, CAP], F32R) for i in range(HR)]
        hid_lo = [sb(f"hid_lo{i}", [P, CAP], F32R) for i in range(HR)]
        outT = qT[:].rearrange("p k b c -> p (k b c)")[:, 0:HALVES * 2 * CAP].rearrange("p (k s) -> p k s", k=HALVES)
        rows = kv_space[:, 0:TPP * DM].rearrange("p (t d) -> p t d", t=TPP)
        zeros = sb("zeros", [P, DM])
        picks = [ctx_sb[:]] + [t[:].rearrange("p k b c -> p (k b c)").rearrange("p (b d) -> p b d", b=B)
                               for t in (attnT, ctxT)]

        bank = [ps(f"bank{i}", [P, 512]) for i in range(8)]
        conv_bank = bank[0:4]
        turn_bank = [bank[4], bank[5], bank[2], bank[3]]
        x2_bank = [bank[6], bank[7], bank[4], bank[5]]
        gate_bank = bank[0]
        pos_bank = bank[1]
        up_bank = bank[0:2]
        down_bank = [bank[2:4], bank[4:6]]
        back_bank = bank[6]
        turn_in = bank[7]

        def by_pair(t):
            return t.rearrange("p (b j i) -> p b j i", b=B, j=HEAD_DIM)

        def queries(h, half):
            return qT[:, half, :, bass.ds(HEAD_DIM * h, HEAD_DIM)].unsqueeze(2).broadcast_to(
                [P, B, HEAD_DIM, HEAD_DIM])

        QUADS = [(slice(None), slice(None), slice(0, HB), slice(0, HEAD_DIM)),
                 (slice(None), slice(None), slice(HB, HEAD_DIM), slice(HB, HEAD_DIM))]

        POOL_ITEM = 3
        POOL_LAG = 2

        kern_loaded = sem("kern_loaded")
        ctx_loaded = [sem(f"ctx_loaded{q}") for q in range(2)]
        x_loaded = [sem(f"x_loaded{q}") for q in range(2)]
        consts_loaded = sem("consts_loaded")
        kern_padded = sem("kern_padded")
        kern_in_dram = [sem(f"kern_in_dram{j}") for j in range(H // SKEW)]
        toep_loaded = [sem(f"toep_loaded{i}") for i in range(HEAD_RING)]
        w_loaded = [[sem(f"w{m}_loaded{a}") for m in (1, 2)] for a in range(2)]
        consts_made = sem("consts_made")
        dve_step = sem("dve_step")
        pool_step = sem("pool_step")
        act_step = sem("act_step")
        turned = sem("turned")
        turn_out = sem("turn_out")
        variance_ready = sem("variance_ready")
        rstd_ready = sem("rstd_ready")
        shift_ready = sem("shift_ready")
        queries_gated = sem("queries_gated")
        gate_centered = sem("gate_centered")
        old_logits_ready = sem("old_logits_ready")
        gate_scaled = sem("gate_scaled")
        q_ready = sem("q_ready")
        kv_ready = sem("kv_ready")
        kv_used = sem("kv_used")
        conv_ready = sem("conv_ready")
        conv_kept = sem("conv_kept")
        multiplied = sem("multiplied")
        pool_multiplied = sem("pool_multiplied")
        summed = sem("summed")
        x2_ready = sem("x2_ready")
        x2_kept = sem("x2_kept")
        xn_ready = [sem(f"xn_ready{q}") for q in range(2)]
        xn_stored = sem("xn_stored")
        gated = sem("gated")
        tanh_ready = sem("tanh_ready")
        shifted = sem("shifted")
        exp_ready = sem("exp_ready")
        taken_ready = sem("taken_ready")
        positions_ready = sem("positions_ready")
        slot_col_ready = sem("slot_col_ready")
        tiles_found = sem("tiles_found")
        tiles_marked = sem("tiles_marked")
        dve_hots = sem("dve_hots")
        pool_hots = sem("pool_hots")
        table_ready = sem("table_ready")
        rows_known = sem("rows_known")
        first_rows = [sem(f"first_rows{t}") for t in range(3)]
        gather_a = sem("gather_a")
        gather_b = sem("gather_b")
        in_turned = sem("in_turned")
        in_hi_ready = sem("in_hi_ready")
        in_lo_ready = sem("in_lo_ready")
        w_hi_ready = sem("w_hi_ready")
        w1_lo_ready = sem("w1_lo_ready")
        w2_lo_ready = sem("w2_lo_ready")
        up_done = sem("up_done")
        down_done = sem("down_done")
        hid_ready = sem("hid_ready")
        hid_hi_ready = sem("hid_hi_ready")
        hid_lo_ready = sem("hid_lo_ready")
        outT_ready = sem("outT_ready")
        first_half_done = sem("first_half_done")
        second_half_ready = sem("second_half_ready")
        out_turned = sem("out_turned")
        row_ready = sem("row_ready")
        scattered = sem("scattered")
        last_scattered = sem("last_scattered")
        zeroed = sem("zeroed")
        picks_zeroed = sem("picks_zeroed")
        picks_loaded = [sem(f"picks_loaded{q}") for q in range(ENDS)]
        last_loaded = [sem(f"last_loaded{q}") for q in range(ENDS)]
        first_added = sem("first_added")
        second_added = sem("second_added")
        result_ready = sem("result_ready")
        stored = sem("stored")

        in_bank = [turn_in, back_bank]

        def row_bank(t, alone):
            return turn_in if alone and t % 2 else back_bank

        INPUTS_AT = (2, 6)
        SPLITS_AT = 2

        BACK_AT = 2

        PIECES = 4
        PW = HALVES * HID // PIECES

        def w1_block(t, k, c):
            return t[:, k * HID + c * P:k * HID + (c + 1) * P]

        def w2_block(t, c, m):
            return t[:, c * DM + m * P:c * DM + (m + 1) * P]

        block = stack.enter_context(nc.Block())

        @block.sync
        def _(sp):
            sp.dma_start(kern_sb[:, P:P + L], ssm_kernel).then_inc(kern_loaded, 16)
            sp.dma_start(D_sb[:], D_skip.rearrange("(h a) -> h a", a=1)).then_inc(kern_loaded, 16)
            for q in range(2):
                part = slice(q * GB, (q + 1) * GB)
                sp.dma_start(x_sb[:, part, :], x[part].rearrange("b s d -> s b d")).then_inc(x_loaded[q], 16)
            for q in range(2):
                part = slice(q * GB, (q + 1) * GB)
                sp.dma_start(ctx_sb[:, part, :], ctx[part].rearrange("b s d -> s b d")).then_inc(ctx_loaded[q], 16)
            sp.wait_ge(kern_padded, 1)

            def skew(n):
                heads = slice(SKEW * n, SKEW * (n + 1))
                dst = bass.AP(skewed.tensor, SKEW * n * P * (ROW + 1),
                              [[P * (ROW + 1), SKEW], [ROW + 1, P], [1, ROW]])
                sp.dma_start(dst, kern_sb[heads, :].unsqueeze(1).broadcast_to([SKEW, P, ROW])
                             ).then_inc(kern_in_dram[n], 16)

            def load_toeplitz(j, ring, meanwhile=()):
                for i in range(HEAD_RING):
                    if isinstance(j, int) and i % SKEW == 0:
                        sp.wait_ge(kern_in_dram[(HEAD_RING * j + i) // SKEW], 16)
                    if ring:
                        sp.wait_ge(kv_used, HEAD_RING * (j - 1) + i + 1)
                    src = skewed[bass.ds(HEAD_RING * j + i, 1), 0:P * ROW].rearrange("a (m l) -> (a m) l", m=P)
                    sp.dma_start(toep[i][:], src[:, P:P + L]).then_inc(toep_loaded[i], 16)
                    if i < len(meanwhile):
                        skew(meanwhile[i])

            skew(0)
            skew(1)
            sp.dma_start(gates2[:, 0:1], g_xattn.rearrange("(a b) -> a b", a=1).broadcast_to([P, 1])
                         ).then_inc(consts_loaded, 16)
            sp.dma_start(gates2[:, 1:2], g_ffn.rearrange("(a b) -> a b", a=1).broadcast_to([P, 1])
                         ).then_inc(consts_loaded, 16)
            sp.dma_start(gate_sb[:], gating_w.rearrange("(k p) e -> p k e", p=P)).then_inc(consts_loaded, 16)
            sp.dma_start(bias_rows[0:E * CH, :], b1.rearrange("e (c p) -> (e c) p", p=P)).then_inc(consts_loaded, 16)
            sp.dma_start(bias_rows[E * CH:, :], b2.rearrange("e (c p) -> (e c) p", p=P)).then_inc(consts_loaded, 16)
            load_toeplitz(0, False)
            skew(2)
            skew(3)
            load_toeplitz(1, True, meanwhile=range(4, H // SKEW))

            def load_weights(g, a):
                n = 2 * g + a
                sp.dma_start(w_raw[a][0][:].rearrange("p (k h) -> p k h", k=HALVES),
                             w1[bass.ds(n, 1)].rearrange("e (k p) h -> p (e k) h", p=P)
                             ).then_inc(w_loaded[a][0], 16)
                sp.dma_start(w_raw[a][1][:].rearrange("p (c d) -> p c d", c=CH),
                             w2[bass.ds(n, 1)].rearrange("e (c p) d -> p (e c) d", p=P)
                             ).then_inc(w_loaded[a][1], 16)

            for n in range(4, H // SKEW):
                sp.wait_ge(kern_in_dram[n], 16)
            with sp.Fori(2, HEAD_LOOPS) as j:
                load_toeplitz(j, True)
            load_weights(0, 0)
            sp.wait_ge(zeroed, 1)
            for k in range(PLANES):
                sp.dma_start(picks_dram[k * T:(k + 1) * T].rearrange("(b s) d -> s b d", s=S),
                             zeros[:].unsqueeze(1).broadcast_to([P, B, DM])
                             ).then_inc(picks_zeroed, 16)
            for q in range(2):
                part = slice(q * GB, (q + 1) * GB)
                sp.wait_ge(xn_ready[q], GB)
                sp.dma_start(tokens_dram.rearrange("(b s) d -> s b d", s=S)[:, part, :], xn_sb[:, part, :]
                             ).then_inc(xn_stored, 16)
            sp.wait_ge(summed, HALVES * H)
            load_weights(0, 1)
            with sp.Fori(1, PAIRS) as g:
                for a in range(2):
                    sp.wait_ge(w1_lo_ready, PIECES * (2 * g + a - 1))
                    sp.wait_ge(w2_lo_ready, PIECES * (2 * g + a - 1))
                    load_weights(g, a)

            def load_picks(k, q, semaphore):
                part = slice(q * EB, (q + 1) * EB)
                src = picks_dram[k * T:(k + 1) * T].rearrange("(b s) d -> s b d", s=S)
                sp.dma_start(picks[k][:, part, :], src[:, part, :]).then_inc(semaphore, 16)

            sp.wait_ge(scattered, 16 * EARLY)
            for q in range(ENDS):
                for k in range(TOP_K):
                    load_picks(k, q, picks_loaded[q])
            sp.wait_ge(last_scattered, 16 * (TILES + 1 - EARLY))
            for q in range(ENDS):
                load_picks(TOP_K, q, last_loaded[q])
            for q in range(ENDS):
                part = slice(q * EB, (q + 1) * EB)
                sp.wait_ge(result_ready, EB * (q + 1))
                sp.dma_start(out[part].rearrange("b s d -> s b d"), xn_sb[:, part, :]).then_inc(stored, 16)
            sp.wait_ge(stored, 16 * ENDS)

        @block.gpsimd
        def _(pool):
            nc.gpsimd.memset(ident[:], 0.0).then_inc(pool_step, 1)
            nc.gpsimd.memset(ones[:], 1.0).then_inc(pool_step, 1)
            pool.wait_ge(pool_step, 2)
            nc.gpsimd.affine_select(out=ident[:], in_=ident[:], pattern=[[-1, P]], compare_op=ALU.not_equal,
                                    fill=1.0, base=0, channel_multiplier=1).then_inc(consts_made, 1)
            nc.gpsimd.affine_select(out=before[:], in_=ones[:], pattern=[[1, P]], compare_op=ALU.is_gt,
                                    fill=0.0, base=0, channel_multiplier=-1).then_inc(consts_made, 1)
            nc.gpsimd.iota(expert_iota[:], [[1, E]], base=0, channel_multiplier=0,
                           allow_small_or_imprecise_dtypes=True).then_inc(consts_made, 1)
            nc.gpsimd.iota(tile_iota[:], [[1, TILES]], base=0, channel_multiplier=0,
                           allow_small_or_imprecise_dtypes=True).then_inc(consts_made, 1)
            nc.gpsimd.iota(col_iota[:], [[1, P]], base=0, channel_multiplier=0,
                           allow_small_or_imprecise_dtypes=True).then_inc(consts_made, 1)
            nc.gpsimd.iota(item_id[:], [[S, B], [T, TOP_K]], base=1, channel_multiplier=1,
                           allow_small_or_imprecise_dtypes=True).then_inc(consts_made, 1)
            nc.gpsimd.memset(minus_half[:], -0.5).then_inc(pool_step, 1)
            nc.gpsimd.memset(ones_f, 1.0).then_inc(consts_made, 1)
            nc.gpsimd.memset(zeros[:], 0.0).then_inc(zeroed, 1)

            def make_kv(j, first):
                for i in range(HEAD_RING):
                    h = HEAD_RING * j + i
                    if not first or i >= KV_RING:
                        pool.wait_ge(kv_used, h - KV_RING + 1)
                    for half in range(HALVES):
                        if first and i == 0:
                            pool.wait_ge(turn_out, 2 * (half + 1))
                        c = ctxT[:, half, :, bass.ds(HEAD_DIM * h, HEAD_DIM)]
                        quads = by_pair(kv[i % KV_RING][:, half, :])
                        for quad in QUADS:
                            rows_of, cols_of = quad[2:]
                            shape = [P, B, HB, cols_of.stop - cols_of.start]
                            last = nc.gpsimd.tensor_tensor(
                                quads[quad],
                                c[:, :, rows_of].unsqueeze(3).broadcast_to(shape),
                                c[:, :, cols_of].unsqueeze(2).broadcast_to(shape), ALU.mult)
                        last.then_inc(kv_ready, 1)
                        if half == 0 and HALVES * (i - POOL_LAG) + 1 == POOL_ITEM:
                            k = POOL_ITEM % PROD_RING
                            pool.wait_ge(conv_kept, HALVES * (h - POOL_LAG + 1))
                            nc.gpsimd.tensor_tensor(by_pair(prod[k]), by_pair(prod[k]), queries(h - POOL_LAG, 1),
                                                    ALU.mult).then_inc(pool_multiplied, 1)

            def inverse_deviation(count):
                pool.wait_ge(variance_ready, count)
                group = slice(GB * ((count - 1) % 2), GB * ((count - 1) % 2 + 1))
                nc.gpsimd.tensor_tensor(rstd[:, group], rstd[:, group], minus_half[:, group], ALU.pow
                                        ).then_inc(rstd_ready, 1)

            pool.wait_ge(pool_step, 3)
            inverse_deviation(1)
            inverse_deviation(2)
            make_kv(0, True)
            with pool.Fori(1, HEAD_LOOPS) as j:
                make_kv(j, False)

            def w2_piece(n, a, q):
                pool.wait_ge(w_hi_ready, 2 * PIECES * n + PIECES + q + 1)
                cols = slice(q * PW, (q + 1) * PW)
                nc.gpsimd.tensor_tensor(w_lo[a][1][:, cols], w_raw[a][1][:, cols],
                                        w_hi[a][1][:, cols].bitcast(F32), ALU.subtract).then_inc(w2_lo_ready, 1)

            last_token = nc.gpsimd.to_reg(T - 1)
            last_pick = nc.gpsimd.to_reg(PLANES * T - 1)

            def gather(g, tiles):
                for t in tiles:
                    nc.gpsimd.indirect_dma_start(
                        gathered[:, t, :], None, tokens_dram,
                        bass.IndirectOffsetOnAxis(ap=source_row[:, TPP * g + t:TPP * g + t + 1], axis=0),
                        bounds_check=last_token, oob_is_err=False
                        ).then_inc(gather_b if t >= 3 else first_rows[t] if g == 0 else gather_a, 16)

            def scatter(g, t, slots=P, targets=None, count=None, done=scattered):
                pool.wait_ge(row_ready, count or TPP * g + t + 1)
                if targets is None:
                    targets = target_row[0:slots, TPP * g + t:TPP * g + t + 1]
                nc.gpsimd.indirect_dma_start(
                    picks_dram, bass.IndirectOffsetOnAxis(ap=targets, axis=0), rows[0:slots, t, :], None,
                    bounds_check=last_pick, oob_is_err=False).then_inc(done, 16)

            for q in range(2):
                inverse_deviation(3 + q)
                pool.wait_ge(rstd_ready, 3 + q)
                part = slice(q * GB, (q + 1) * GB)
                nc.gpsimd.tensor_tensor(shift[:, part], neg_mean[:, part], rstd[:, part], ALU.mult
                                        ).then_inc(shift_ready, 1)
            for q in range(PIECES):
                w2_piece(0, 0, q)
            pool.wait_ge(tiles_found, 1)
            nc.gpsimd.tensor_tensor(tile_ids[:], tile_hot[:],
                                    item_id[:].rearrange("p b k -> p (b k)").unsqueeze(2).broadcast_to([P, NR, TILES]),
                                    ALU.mult).then_inc(tiles_marked, 1)
            pool.wait_ge(slot_col_ready, 1)
            for r in range(NR - POOL_HOTS, NR):
                nc.gpsimd.tensor_scalar(col_hot[:, r, :], col_iota[:], slot_col[:, r // TOP_K, r % TOP_K:r % TOP_K + 1], None,
                                        ALU.is_equal).then_inc(pool_hots, 1)
            pool.wait_ge(xn_stored, 16 * 2)
            pool.wait_ge(rows_known, 1)
            gather(0, range(TPP))
            pool.wait_ge(rows_known, 4)
            pool.wait_ge(picks_zeroed, 16 * PLANES)
            for g in range(PAIRS):
                for q in range(PIECES):
                    if g > 0 and q < TPP - 2:
                        scatter(g - 1, 2 + q)
                    w2_piece(2 * g + 1, 1, q)
                if g < PAIRS - 1:
                    pool.wait_ge(in_turned, HALVES * (2 * g + 2))
                    gather(g + 1, range(TPP))
                for q in range(PIECES):
                    if q < 2:
                        scatter(g, q)
                    if g < PAIRS - 1:
                        w2_piece(2 * g + 2, 0, q)
            scatter(PAIRS - 1, 2, slots=P // 2)
            scatter(PAIRS - 1, 2, targets=half_targets[:], count=EARLY + 1, done=last_scattered)
            for t in range(3, TPP):
                scatter(PAIRS - 1, t, count=EARLY + t - 1, done=last_scattered)

        @block.tensor
        def _(pe):
            def turn(use, src, half, b0):
                wait_for(pe, turn_out, use - 3)
                for q in range(4):
                    b = b0 + q
                    last = pe.transpose(turn_bank[use % 4][:, q * P:(q + 1) * P],
                                        src[:, b, half * P:(half + 1) * P], ident[:])
                last.then_inc(turned, 1)

            def place_x(batches):
                pe.wait_ge(x_loaded[batches[0] // GB], 16)
                for b in batches:
                    pe.matmul(x2_bank[b // 2][:, (b % 2) * DM:(b % 2 + 1) * DM], ident[:], x_sb[:, b, :],
                              start=(b % 2 == 0), stop=False, skip_group_check=True)

            pe.wait_ge(consts_made, 1)
            place_x(range(GB))
            use = 0
            for half in range(HALVES):
                for b0 in (0, GB):
                    pe.wait_ge(ctx_loaded[b0 // GB], 16)
                    turn(use, ctx_sb, half, b0)
                    use += 1
            for b0 in (0, GB):
                pe.wait_ge(q_ready, b0 + GB)
                for half in range(HALVES):
                    turn(use, xn_sb, half, b0)
                    use += 1

            def gate_queries(batches):
                for b in batches:
                    for half in range(HALVES):
                        last = pe.matmul(turn_bank[1][:, b * E:(b + 1) * E], qT[:, half, b, :], gate_sb[:, half, :],
                                         start=False, stop=(half == 1), skip_group_check=True)
                last.then_inc(queries_gated, 1)

            def convolve(j, first, last=False):
                for i in range(HEAD_RING):
                    h = HEAD_RING * j + i
                    pe.wait_ge(toep_loaded[i], 16 * (j + 1))
                    if first and i == 1:
                        pe.wait_ge(turn_out, 8)
                    y0, y1 = conv_bank[2 * (i % 2)], conv_bank[2 * (i % 2) + 1]
                    if not first or i >= 2:
                        pe.wait_ge(conv_kept, HALVES * (h - 1))
                    for y, taps, half in ((y0, slice(0, P), 0), (y1, slice(P, L), 0), (y1, slice(0, P), 1)):
                        if taps.start == 0:
                            pe.wait_ge(kv_ready, HALVES * h + half + 1)
                        for q, quad in enumerate(QUADS):
                            product = pe.matmul(by_pair(y[:])[quad], toep[i][:, taps],
                                                by_pair(kv[i % KV_RING][:, half, :])[quad],
                                                start=(half == 0 and q == 0), stop=True, skip_group_check=True)
                        if y is y0:
                            product.then_inc(conv_ready, 1)
                    product.then_inc(kv_used, 1)
                    if last:
                        gate_queries(range(2 * i, 2 * i + 2))

            convolve(0, True)
            with pe.Fori(1, HEAD_LOOPS - 1) as j:
                convolve(j, False)
            pe.wait_ge(consts_loaded, 16 * 5)
            NB = E * (CH + HALVES)
            pe.transpose(turn_bank[0][:, 0:NB], bias_rows[:], ident[0:NB, 0:NB]).then_inc(turned, 1)
            pe.wait_ge(consts_made, 7)
            for half in range(HALVES):
                last = pe.matmul(turn_bank[1][:, B * E:(B + 1) * E], ones_f, gate_sb[:, half, :],
                                 start=(half == 0), stop=(half == HALVES - 1), skip_group_check=True)
            convolve(HEAD_LOOPS - 1, False, last=True)

            pe.wait_ge(act_step, 1)
            place_x(range(GB, GB + 2))
            pe.wait_ge(act_step, 2)
            place_x(range(GB + 2, B))
            pe.wait_ge(gate_scaled, 1)
            for half in range(HALVES):
                pe.wait_ge(summed, HALVES * H if half else HALVES * H - 2)
                for b in range(B):
                    col = (b % 2) * DM + half * P
                    last = pe.matmul(x2_bank[b // 2][:, col:col + P], attnT[:, half, b, :], scaled_ident,
                                     start=False, stop=(half == 1), skip_group_check=True)
                    if half == 1 and b % 2 == 1:
                        last.then_inc(x2_ready, 1)
            pe.wait_ge(gate_scaled, 2)
            for b in range(B):
                for half in range(HALVES):
                    last = pe.matmul(gate_bank[:, b * E:(b + 1) * E], attnT[:, half, b, :], scaled_gate[:, half, :],
                                     start=(b == half == 0), stop=(half == 1), skip_group_check=True)
            last.then_inc(gated, 1)

            pe.wait_ge(taken_ready, 1)
            flat = taken[:].rearrange("p b e -> p (b e)")
            for b in range(B - 1):
                pe.matmul(pos_bank[:, (b + 1) * E:B * E], ones[:],
                          taken[:, b:b + 1, :].broadcast_to([P, B - 1 - b, E]),
                          start=(b == 0), stop=False, skip_group_check=True)
            pe.matmul(pos_bank[:, 0:B * E], before[:], flat, start=False, stop=True, skip_group_check=True
                      ).then_inc(positions_ready, 1)
            pe.wait_ge(tiles_marked, 1)
            for r in range(NR):
                if r < NR - POOL_HOTS:
                    pe.wait_ge(dve_hots, r + 1)
                else:
                    pe.wait_ge(pool_hots, r - (NR - POOL_HOTS) + 1)
                last = pe.matmul(gate_bank[:, 128:128 + TILES], col_hot[:, r, :], tile_ids[:, r, :],
                                 start=(r == 0), stop=(r == NR - 1))
            last.then_inc(table_ready, 1)

            def first_inputs():
                for t, count in enumerate((P, P, P // 2)):
                    pe.wait_ge(first_rows[t], 16)
                    for half in range(HALVES):
                        last = pe.transpose(in_bank[half][:, t * P:t * P + count],
                                            gathered[0:count, t, half * P:(half + 1) * P], ident[0:count, 0:count])
                        if t == 2:
                            last.then_inc(in_turned, 1)

            def inputs(g, a, half):
                if half == 0:
                    if a == 0:
                        pe.wait_ge(gather_a, 16 * 3 * g)
                    else:
                        pe.wait_ge(gather_b, 16 * 2 * (g + 1))
                wait_for(pe, in_lo_ready, HALVES * (2 * g + a))
                if half == 1:
                    wait_for(pe, row_ready, TPP * g - 3)
                if a == 0:
                    pieces = [(0, 0, P, 0), (1, 0, P, P), (2, 0, P // 2, 2 * P)]
                else:
                    pieces = [(3, 0, P, P // 2), (4, 0, P, P // 2 + P), (2, P // 2, P, 0)]
                for t, p0, p1, col in pieces:
                    last = pe.transpose(in_bank[half][:, col:col + p1 - p0],
                                        gathered[p0:p1, t, half * P:(half + 1) * P], ident[p0:p1, p0:p1])
                last.then_inc(in_turned, 1)

            def up(n, a, c):
                if c == 0:
                    pe.wait_ge(w_hi_ready, 2 * PIECES * n + PIECES)
                wait_for(pe, hid_ready, CH * n + c - 1)
                bankc = up_bank[c % 2][:, 0:CAP]
                for k in range(HALVES):
                    hi, lo = w1_block(w_hi[a][0], k, c), w1_block(w_lo[a][0], k, c)
                    if c == 0:
                        pe.wait_ge(in_hi_ready, HALVES * n + k + 1)
                    pe.matmul(bankc, hi, in_hi[a][:, k, :], start=(k == 0), stop=False)
                    if c == 0:
                        pe.wait_ge(in_lo_ready, HALVES * n + k + 1)
                    pe.matmul(bankc, hi, in_lo[a][:, k, :], start=False, stop=False)
                    if c == 0 and k == 0:
                        pe.wait_ge(w1_lo_ready, PIECES * (n + 1))
                    last = pe.matmul(bankc, lo, in_hi[a][:, k, :], start=False, stop=(k == HALVES - 1))
                last.then_inc(up_done, 1)

            def down(n, a, c, ends=False):
                if c == 0:
                    pe.wait_ge(w_hi_ready, 2 * PIECES * (n + 1))
                    pe.wait_ge(w2_lo_ready, PIECES * (n + 1))
                    wait_for(pe, outT_ready, n - 1)
                pe.wait_ge(hid_lo_ready, CH * n + c + 1)
                for m in range(HALVES):
                    hi, lo = w2_block(w_hi[a][1], c, m), w2_block(w_lo[a][1], c, m)
                    bankm = down_bank[a][m][:, 0:CAP]
                    pe.matmul(bankm, hi, hid_hi[c % HR][:], start=(c == 0), stop=False)
                    pe.matmul(bankm, hi, hid_lo[c % HR][:], start=False, stop=False)
                    last = pe.matmul(bankm, lo, hid_hi[c % HR][:], start=False, stop=(c == CH - 1))
                    if ends and m == 0:
                        last.then_inc(first_half_done, 1)
                last.then_inc(down_done, 1)

            def back(g, t, alone=False, cols=P):
                if t == 0:
                    pe.wait_ge(outT_ready, 2 * g + 1)
                if t == 2 and cols == P:
                    pe.wait_ge(outT_ready, 2 * g + 2)
                if t == 2 and not alone and cols == P:
                    pe.wait_ge(in_lo_ready, HALVES * (2 * g + 4))
                wait_for(pe, row_ready, TPP * g + (max(t, 3) if alone else t))
                for half in range(HALVES):
                    if alone and half == 1:
                        pe.wait_ge(second_half_ready, 1)
                    last = pe.transpose(row_bank(t, alone)[0:cols, half * P:(half + 1) * P],
                                        outT[:, half, t * P:t * P + cols], ident[:])
                last.then_inc(out_turned, 1)

            def pair(g, first, last):
                for a in range(2):
                    n = 2 * g + a
                    for c in range(CH):
                        up(n, a, c)
                        if c >= 2:
                            down(n, a, c - 2)
                        elif a == 1 or not first:
                            down(n - 1, 1 - a, c + CH - 2)
                        if a == 0 and not first and 3 <= c < 6:
                            back(g - 1, c - 1)
                        if a == 1 and BACK_AT <= c < BACK_AT + 2:
                            back(g, c - BACK_AT)
                        if a == 1 and last and c == BACK_AT + 2:
                            back(g, 2, cols=P // 2)
                        if c == INPUTS_AT[a] and not (last and a == 1):
                            for half in range(HALVES):
                                inputs(g + a, 1 - a, half)

            pe.wait_ge(rows_known, 4)
            pe.wait_ge(x2_kept, B // 2)
            first_inputs()
            pair(0, True, False)
            with pe.Fori(1, PAIRS - 1) as g:
                pair(g, False, False)
            pair(PAIRS - 1, False, True)
            down(E - 1, 1, CH - 2)
            down(E - 1, 1, CH - 1, ends=True)
            for t in range(2, TPP):
                back(PAIRS - 1, t, alone=True)

        @block.scalar
        def _(act):
            for use in range(8):
                dst, half, b0 = (ctxT, use // 2, GB * (use % 2)) if use < 4 else (qT, use % 2, GB * (use // 2 - 2))
                act.wait_ge(turned, use + 1)
                nc.scalar.copy(dst[:, half, b0:b0 + GB, :].rearrange("p b c -> p (b c)"),
                               turn_bank[use % 4][:]).then_inc(turn_out, 1)
            act.wait_ge(consts_loaded, 16 * 5)
            nc.scalar.activation(tanh2[:], gates2[:], ACT.Tanh).then_inc(tanh_ready, 1)
            act.wait_ge(tanh_ready, 1)
            nc.scalar.activation(scaled_ident, ident[:], ACT.Identity, scale=tanh2[:, 0:1]).then_inc(gate_scaled, 1)
            def keep(j, first):
                for k in range(HALVES * HEAD_RING):
                    h = HEAD_RING * j + k // HALVES
                    act.wait_ge(kv_used if k % HALVES else conv_ready, h + 1)
                    if not first or k >= PROD_RING:
                        act.wait_ge(summed, HALVES * HEAD_RING * j + k - PROD_RING + 1)
                    y, kept = by_pair(conv_bank[k % 4][:]), by_pair(prod[k % PROD_RING])
                    nc.scalar.copy(kept[:, :, 0:HB, :], y[:, :, 0:HB, :])
                    nc.scalar.copy(kept[:, :, HB:, :], y[:, :, :, HB:].rearrange("p b i j -> p b j i")
                                   ).then_inc(conv_kept, 1)

            keep(0, True)
            with act.Fori(1, HEAD_LOOPS - 1) as j:
                keep(j, False)
            act.wait_ge(turned, 9)
            nc.scalar.copy(biasT[:], turn_bank[0][:, 0:E * (CH + HALVES)]).then_inc(act_step, 1)
            keep(HEAD_LOOPS - 1, False)
            act.wait_ge(queries_gated, HEAD_RING)
            nc.scalar.copy(gate_parts[:].rearrange("p b e -> p (b e)"), turn_bank[1][:, 0:(B + 1) * E]
                           ).then_inc(act_step, 1)

            def split(g, a, piece):
                m, q = piece // PIECES, piece % PIECES
                n = 2 * g + a
                if q == 0:
                    act.wait_ge(w_loaded[a][m], 16 * (g + 1))
                    if m == 0:
                        wait_for(act, up_done, CH * (n - 1))
                    else:
                        wait_for(act, down_done, CH * (n - 1))
                cols = slice(q * PW, (q + 1) * PW)
                nc.scalar.copy(w_hi[a][m][:, cols], w_raw[a][m][:, cols]).then_inc(w_hi_ready, 1)

            def input_high(g, a, half):
                n2 = 2 * (2 * g + a) + half
                act.wait_ge(in_turned, n2 + 1)
                if half == 0:
                    wait_for(act, up_done, CH * (2 * g + a - 1))
                nc.scalar.copy(in_hi[a][:, half, :], in_bank[half][:, 0:CAP]).then_inc(in_hi_ready, 1)

            def hidden(n, c):
                act.wait_ge(up_done, CH * n + c + 1)
                wait_for(act, hid_lo_ready, CH * n + c - 1)
                nc.scalar.activation(hid[c % 2][:], up_bank[c % 2][:, 0:CAP], ACT.Relu,
                                     bias=biasT[:, bass.ds(CH * n + c, 1)]).then_inc(hid_ready, 1)

            def output(n, a, g):
                act.wait_ge(down_done, CH * (n + 1))
                wait_for(act, out_turned, TPP * g)
                for m in range(HALVES):
                    last = nc.scalar.activation(outT[:, m, a * CAP:(a + 1) * CAP], down_bank[a][m][:, 0:CAP],
                                                ACT.Identity, bias=biasT[:, bass.ds(E * CH + HALVES * n + m, 1)])
                last.then_inc(outT_ready, 1)

            for piece in range(2 * PIECES):
                split(0, 0, piece)
            act.wait_ge(gate_centered, 1)
            nc.scalar.activation(scaled_gate[:], gate_c[:], ACT.Identity, scale=tanh2[:, 0:1]
                                 ).then_inc(gate_scaled, 1)
            def normalize(q):
                act.wait_ge(shift_ready, q + 1)
                for b in range(q * GB, (q + 1) * GB):
                    nc.scalar.activation(xn_sb[:, b, :], x2_bank[b // 2][:, (b % 2) * DM:(b % 2 + 1) * DM],
                                         ACT.Identity, bias=shift[:, b:b + 1], scale=rstd[:, b:b + 1]
                                         ).then_inc(xn_ready[q], 1)

            normalize(0)
            act.wait_ge(shifted, 1)
            nc.scalar.activation(probs[:], logits[:], ACT.Exp).then_inc(exp_ready, 1)
            normalize(1)
            for i in range(B // 2):
                nc.scalar.copy(x_sb[:, 2 * i:2 * i + 2, :].rearrange("p b d -> p (b d)"), x2_bank[i][:]
                               ).then_inc(x2_kept, 1)
            act.wait_ge(act_step, 1)
            input_high(0, 0, 0)
            input_high(0, 0, 1)

            def pair(g, first, last):
                for a in range(2):
                    n = 2 * g + a
                    for c in range(CH):
                        hidden(n, c)
                        if c == 1 and (a == 1 or not first):
                            output(n - 1, 1 - a, g if a == 1 else g - 1)
                        if c >= 1 and not (last and a == 1):
                            g2, a2 = (g, 1) if a == 0 else (g + 1, 0)
                            if c == INPUTS_AT[a]:
                                for half in range(HALVES):
                                    input_high(g2, a2, half)
                            if 0 <= c - SPLITS_AT < PIECES:
                                split(g2, a2, 2 * (c - SPLITS_AT))
                                split(g2, a2, 2 * (c - SPLITS_AT) + 1)

            pair(0, True, False)
            with act.Fori(1, PAIRS - 1) as g:
                pair(g, False, False)
            pair(PAIRS - 1, False, True)
            act.wait_ge(first_half_done, 1)
            act.wait_ge(out_turned, TPP * (PAIRS - 1))
            nc.scalar.activation(outT[:, 0, CAP:2 * CAP], down_bank[1][0][:, 0:CAP], ACT.Identity,
                                 bias=biasT[:, E * CH + HALVES * (E - 1):E * CH + HALVES * (E - 1) + 1]
                                 ).then_inc(outT_ready, 1)

        @block.vector
        def _(dve):
            steps = [0]

            def step(ins):
                steps[0] += 1
                ins.then_inc(dve_step, 1)
                dve.wait_ge(dve_step, steps[0])

            step(nc.vector.memset(kern_sb[:, 0:P], 0.0))
            dve.wait_ge(kern_loaded, 32)
            nc.vector.tensor_tensor(kern_sb[:, P:P + 1], kern_sb[:, P:P + 1], D_sb[:], ALU.add
                                    ).then_inc(kern_padded, 1)

            def of_batch(source, b):
                if source is x_sb:
                    return x_sb[:, b, :]
                return source[b // 2][:, (b % 2) * DM:(b % 2 + 1) * DM]

            def statistics(group, source):
                for b in group:
                    if source is not x_sb:
                        dve.wait_ge(x2_ready, b // 2 + 1)
                    last = nc.vector.bn_stats(stats[:, b, :], of_batch(source, b))
                step(last)
                for b in group:
                    last = nc.vector.bn_aggr(moments[:, b, :], stats[:, b, :])
                step(last)
                cols = slice(group[0], group[-1] + 1)
                nc.vector.tensor_scalar(neg_mean[:, cols], moments[:, cols, 0], -1.0, None, ALU.mult)
                nc.vector.tensor_scalar(rstd[:, cols], moments[:, cols, 1], LN_EPS, None, ALU.add
                                        ).then_inc(variance_ready, 1)

            def normalize(group, count, ready):
                dve.wait_ge(rstd_ready, count)
                for b in group:
                    nc.vector.tensor_scalar(xn_sb[:, b, :], x_sb[:, b, :], moments[:, b, 0:1], rstd[:, b:b + 1],
                                            ALU.subtract, ALU.mult).then_inc(ready, 1)

            groups = [range(q * GB, (q + 1) * GB) for q in range(2)]
            for q in range(2):
                dve.wait_ge(x_loaded[q], 16)
                statistics(groups[q], x_sb)
            for q in range(2):
                normalize(groups[q], q + 1, q_ready)
            nc.vector.reciprocal(deviation[:], rstd[:])

            ITEMS = HALVES * HEAD_RING

            def multiply(j, k):
                h, half = HEAD_RING * j + k // HALVES, k % HALVES
                dve.wait_ge(conv_kept, ITEMS * j + k + 1)
                p = by_pair(prod[k % PROD_RING])
                nc.vector.tensor_tensor(p, p, queries(h, half), ALU.mult).then_inc(multiplied, 1)

            def add_up(j, k):
                h, half = HEAD_RING * j + k // HALVES, k % HALVES
                if k == POOL_ITEM:
                    dve.wait_ge(pool_multiplied, j + 1)
                else:
                    dve.wait_ge(multiplied, (ITEMS - 1) * j + k + (1 if k < POOL_ITEM else 0))
                nc.vector.tensor_reduce(attnT[:, half, :, bass.ds(HEAD_DIM * h, HEAD_DIM)],
                                        by_pair(prod[k % PROD_RING]),
                                        AX_X, ALU.add).then_inc(summed, 1)

            def attend(j, first, last=False):
                for k in range(ITEMS):
                    if k != POOL_ITEM:
                        multiply(j, k)
                    if k >= SUM_LAG:
                        add_up(j, k - SUM_LAG)
                    elif not first:
                        add_up(j - 1, ITEMS + k - SUM_LAG)
                    if last and k == ITEMS - 2:
                        add_up(j, ITEMS - 2)

            dve.wait_ge(turn_out, 8)
            attend(0, True)
            with dve.Fori(1, HEAD_LOOPS - 1) as j:
                attend(j, False)
            attend(HEAD_LOOPS - 1, False, last=True)
            add_up(HEAD_LOOPS - 1, ITEMS - 1)
            dve.wait_ge(act_step, 2)
            nc.vector.scalar_tensor_tensor(
                out=gate_c[:], in0=gate_parts[:, B:B + 1, :].broadcast_to([P, HALVES, E]),
                scalar=-1.0 / DM, in1=gate_sb[:], op0=ALU.mult, op1=ALU.add).then_inc(gate_centered, 1)
            of_tokens = [P, B, E]
            nc.vector.tensor_tensor(logits[:], gate_parts[:, 0:B, :],
                                    deviation[:].unsqueeze(2).broadcast_to(of_tokens), ALU.mult
                                    ).then_inc(old_logits_ready, 1)

            for q in range(2):
                statistics(groups[q], x2_bank)

            def w1_split(g, a, q):
                n = 2 * g + a
                dve.wait_ge(w_hi_ready, 2 * PIECES * n + q + 1)
                cols = slice(q * PW, (q + 1) * PW)
                nc.vector.tensor_tensor(w_lo[a][0][:, cols], w_raw[a][0][:, cols],
                                        w_hi[a][0][:, cols].bitcast(F32), ALU.subtract).then_inc(w1_lo_ready, 1)

            dve.wait_ge(gated, 1)
            dve.wait_ge(old_logits_ready, 1)
            bc = of_tokens
            step(nc.vector.tensor_tensor(logits[:], gate_bank[:, 0:B * E].rearrange("p (b e) -> p b e", b=B),
                                         logits[:], ALU.add))
            dve.wait_ge(rstd_ready, 4)
            step(nc.vector.tensor_tensor(logits[:], logits[:], rstd[:].unsqueeze(2).broadcast_to(bc), ALU.mult))
            step(nc.vector.tensor_reduce(small[:, 0, :], logits[:], AX_X, ALU.max))
            nc.vector.tensor_tensor(logits[:], logits[:], small[:, 0, :].unsqueeze(2).broadcast_to(bc), ALU.subtract
                                    ).then_inc(shifted, 1)
            dve.wait_ge(exp_ready, 1)
            step(nc.vector.tensor_reduce(small[:, 1, :], probs[:], AX_X, ALU.add))
            step(nc.vector.reciprocal(small[:, 2, :], small[:, 1, :]))
            step(nc.vector.tensor_tensor(probs[:], probs[:], small[:, 2, :].unsqueeze(2).broadcast_to(bc), ALU.mult))
            for b in range(B):
                last = nc.vector.max(top8[:, b, :], probs[:, b, :])
            step(last)
            for b in range(B):
                last = nc.vector.max_index(top8_at[:, b, :], top8[:, b, :], probs[:, b, :])
            step(last)
            dve.wait_ge(consts_made, 6)
            bke = [P, B, TOP_K, E]
            step(nc.vector.tensor_tensor(onehot[:], top8_at[:, :, 0:TOP_K].unsqueeze(3).broadcast_to(bke),
                                         expert_iota[:].unsqueeze(1).unsqueeze(1).broadcast_to(bke), ALU.is_equal))
            nc.vector.tensor_tensor(taken[:], onehot[:, :, 0], onehot[:, :, 1], ALU.add).then_inc(taken_ready, 1)
            nc.vector.tensor_copy(chosen[:], top8_at[:, :, 0:TOP_K])
            dve.wait_ge(positions_ready, 1)
            pos = pos_bank[:, 0:B * E].rearrange("p (b e) -> p b e", b=B)
            step(nc.vector.tensor_tensor(before_me[:], onehot[:], pos.unsqueeze(2).broadcast_to(bke), ALU.mult))
            step(nc.vector.tensor_reduce(position[:], before_me[:], AX_X, ALU.add))
            nc.vector.tensor_scalar(dropped[:], position[:], float(CAP), OUT_OF_BOUNDS, ALU.is_ge, ALU.mult)
            step(nc.vector.scalar_tensor_tensor(out=slot[:], in0=chosen[:], scalar=float(CAP), in1=position[:],
                                                op0=ALU.mult, op1=ALU.add))
            step(nc.vector.tensor_tensor(slot_i[:], slot[:], dropped[:], ALU.add))
            nc.vector.tensor_scalar(slot_tile_i[:], slot_i[:], 7, None, ALU.logical_shift_right)
            step(nc.vector.tensor_scalar(slot_col_i[:], slot_i[:], P - 1, None, ALU.bitwise_and))
            nc.vector.tensor_copy(slot_col[:], slot_col_i[:]).then_inc(slot_col_ready, 1)
            bt = [P, NR, TILES]
            nc.vector.tensor_tensor(tile_hot[:], slot_tile_i[:].rearrange("p b k -> p (b k)").unsqueeze(2).broadcast_to(bt),
                                    tile_iota[:].unsqueeze(1).broadcast_to(bt), ALU.is_equal).then_inc(tiles_found, 1)
            dve.wait_ge(slot_col_ready, 1)
            for r in range(NR - POOL_HOTS):
                nc.vector.tensor_scalar(col_hot[:, r, :], col_iota[:], slot_col[:, r // TOP_K, r % TOP_K:r % TOP_K + 1], None,
                                        ALU.is_equal).then_inc(dve_hots, 1)
            dve.wait_ge(table_ready, 1)
            table = gate_bank[:, 128:128 + TILES]
            nc.vector.tensor_scalar(table_a[:], table, float(T), -float(T), ALU.is_gt, ALU.mult)
            nc.vector.tensor_scalar(table_b[:], table, 1.0, -1.0, ALU.max, ALU.add)
            step(nc.vector.tensor_scalar(table_c[:], table, 0.0, OUT_OF_BOUNDS, ALU.is_equal, ALU.mult))
            nc.vector.tensor_tensor(source_row[:], table_b[:], table_a[:], ALU.add).then_inc(rows_known, 1)
            dve.wait_ge(rows_known, 1)
            for part, cols in ((slice(P // 2, P), slice(TILES - 3, TILES - 2)), (slice(0, P), slice(TILES - 2, TILES))):
                last = nc.vector.scalar_tensor_tensor(
                    out=table_b[part, cols], in0=table_a[part, cols], scalar=float(TOP_K * T),
                    in1=table_b[part, cols], op0=ALU.add, op1=ALU.add)
            step(last)
            nc.vector.tensor_tensor(target_row[:], table_c[:], table_b[:], ALU.add).then_inc(rows_known, 1)
            low, high, middle = slice(0, P // 2), slice(P // 2, P), slice(TILES - 3, TILES - 2)
            nc.vector.tensor_scalar(half_targets[low, :], table[low, middle], 0.0, OUT_OF_BOUNDS, ALU.mult, ALU.add
                                    ).then_inc(rows_known, 1)
            nc.vector.tensor_tensor(half_targets[high, :], table_c[high, middle], table_b[high, middle], ALU.add
                                    ).then_inc(rows_known, 1)
            both = top8[:, :, 0:TOP_K]
            step(nc.vector.tensor_reduce(small[:, 3, :], both, AX_X, ALU.add))
            step(nc.vector.tensor_scalar(small[:, 3, :], small[:, 3, :], NORM_EPS, None, ALU.add))
            step(nc.vector.reciprocal(small[:, 3, :], small[:, 3, :]))
            nc.vector.tensor_scalar(dropped[:], position[:], float(CAP), tanh2[:, 1:2], ALU.is_lt, ALU.mult)
            step(nc.vector.tensor_tensor(weight[:], both, small[:, 3, :].unsqueeze(2).broadcast_to([P, B, TOP_K]),
                                         ALU.mult))
            step(nc.vector.tensor_tensor(weight[:], weight[:], dropped[:], ALU.mult))
            step(nc.vector.tensor_tensor(last_parts[:], weight[:], onehot[:, :, :, E - 1], ALU.mult))
            nc.vector.tensor_tensor(last_weight[:], last_parts[:, :, 0], last_parts[:, :, 1], ALU.add)
            for q in range(PIECES):
                w1_split(0, 0, q)

            def input_low(g, a, half):
                n2 = 2 * (2 * g + a) + half
                dve.wait_ge(in_hi_ready, n2 + 1)
                nc.vector.tensor_tensor(in_lo[a][:, half, :], in_bank[half][:, 0:CAP],
                                        in_hi[a][:, half, :].bitcast(F32), ALU.subtract).then_inc(in_lo_ready, 1)

            def hidden_split(n, c):
                dve.wait_ge(hid_ready, CH * n + c + 1)
                wait_for(dve, down_done, CH * n + c - HR + 1)
                nc.vector.tensor_copy(hid_hi[c % HR][:], hid[c % 2][:]).then_inc(hid_hi_ready, 1)
                dve.wait_ge(hid_hi_ready, CH * n + c + 1)
                nc.vector.tensor_tensor(hid_lo[c % HR][:], hid[c % 2][:], hid_hi[c % HR][:].bitcast(F32),
                                        ALU.subtract).then_inc(hid_lo_ready, 1)

            def row_tile(g, t, part=slice(0, P), alone=False):
                dve.wait_ge(out_turned, TPP * g + t + (2 if alone else 1))
                if t == 0:
                    wait_for(dve, scattered, 16 * TPP * g)
                nc.vector.tensor_copy(rows[part, t, :], row_bank(t, alone)[part, 0:DM]).then_inc(row_ready, 1)

            input_low(0, 0, 0)
            input_low(0, 0, 1)

            def pair(g, first, last):
                for a in range(2):
                    n = 2 * g + a
                    for c in range(CH):
                        hidden_split(n, c)
                        if a == 0 and not first and 3 <= c < 6:
                            row_tile(g - 1, c - 1)
                        if a == 1 and BACK_AT <= c < BACK_AT + 2:
                            row_tile(g, c - BACK_AT)
                        if a == 1 and last and c == BACK_AT + 2:
                            row_tile(g, 2, slice(0, P // 2))
                        if c >= 1 and not (last and a == 1):
                            g2, a2 = (g, 1) if a == 0 else (g + 1, 0)
                            if c == INPUTS_AT[a]:
                                for half in range(HALVES):
                                    input_low(g2, a2, half)
                            if 0 <= c - SPLITS_AT < PIECES:
                                w1_split(g2, a2, c - SPLITS_AT)

            pair(0, True, False)
            with dve.Fori(1, PAIRS - 1) as g:
                pair(g, False, False)
            pair(PAIRS - 1, False, True)
            dve.wait_ge(down_done, CH * E)
            nc.vector.tensor_scalar(outT[:, 1, CAP:2 * CAP], down_bank[1][1][:, 0:CAP],
                                    biasT[:, E * CH + HALVES * E - 1:E * CH + HALVES * E], None, ALU.add
                                    ).then_inc(second_half_ready, 1)
            row_tile(PAIRS - 1, 2, slice(P // 2, P), alone=True)
            for t in range(3, TPP):
                row_tile(PAIRS - 1, t, alone=True)

            def add_pick(k, b, scale, result, done):
                nc.vector.scalar_tensor_tensor(out=result[:, b, :], in0=picks[k][:, b, :], scalar=scale,
                                               in1=x_sb[:, b, :], op0=ALU.mult, op1=ALU.add).then_inc(done, 1)

            dve.wait_ge(x2_kept, B // 2)
            for q in range(ENDS):
                batches = range(q * EB, (q + 1) * EB)
                dve.wait_ge(picks_loaded[q], 16 * TOP_K)
                for b in batches:
                    add_pick(0, b, weight[:, b, 0:1], x_sb, first_added)
                for b in batches:
                    dve.wait_ge(first_added, b + 1)
                    add_pick(1, b, weight[:, b, 1:2], x_sb, second_added)
            for q in range(ENDS):
                dve.wait_ge(last_loaded[q], 16)
                for b in range(q * EB, (q + 1) * EB):
                    dve.wait_ge(second_added, b + 1)
                    add_pick(TOP_K, b, last_weight[:, b:b + 1], xn_sb, result_ready)


_INS = ['x', 'ctx_2048', 'g_xattn', 'g_ffn', 'L0_xattn_ssm_kernel', 'L0_xattn_D', 'L0_ffn_gating_w',
        'L0_ffn_w1', 'L0_ffn_b1', 'L0_ffn_w2', 'L0_ffn_b2']


def kernel(**inputs):
    import numpy as np
    import concourse.bacc as bacc
    from concourse.bass_utils import run_bass_kernel_spmd

    nc = bacc.Bacc("TRN2", target_bir_lowering=False, num_devices=1)
    arrays, args = {}, []
    for name in _INS:
        a = np.ascontiguousarray(inputs[name])
        arrays[f"in_{name}"] = a
        args.append(nc.dram_tensor(f"in_{name}", a.shape, mybir.dt.from_np(a.dtype), kind="ExternalInput").ap())
    out = nc.dram_tensor("out", arrays["in_x"].shape, F32, kind="ExternalOutput").ap()
    build_gated_block(nc, *args, out)
    result = run_bass_kernel_spmd(nc, [arrays], core_ids=[0])
    return result.results[0]["out"]
```
